# Optimizing a Trainium2 kernel written in Bass

```python
import numpy as np
import jax
import jax.numpy as jnp

def _softmax(x, axis=-1):
    return jax.nn.softmax(x, axis=axis)

def _gelu(x):
    return jax.nn.gelu(x, approximate=True)

def _silu(x):
    return jax.nn.silu(x)

def _sigmoid(x):
    return jax.nn.sigmoid(x)

def _layernorm(x, axis=-1, eps=1e-05):
    m = jnp.mean(x, axis=axis, keepdims=True)
    v = jnp.var(x, axis=axis, keepdims=True)
    return (x - m) / jnp.sqrt(v + eps)

def _scatter_add(tgt, idx, src, axis=0):
    return tgt.at[idx].add(src)

def _segment_sum(src, seg, n):
    return jax.ops.segment_sum(src, seg, n)
kernel_name = 'mk_prb_d1_jaxref_r8_0dc7c0'

def setup_inputs(seed: int=0):
    np.random.seed(seed)
    _w = jnp.asarray

    def _L0_attn_setup():
        import jax, jax.numpy as jnp
        import numpy as np
        HEADS = 16
        DIM_HEAD = 64
        RMS_EPS = 1e-12
        key = jax.random.key(seed)
        k1, k2, k3 = jax.random.split(key, 3)
        b, n, dim = (2, 256, 128)
        dim_inner = HEADS * DIM_HEAD
        x = jax.random.normal(k1, (b, n, dim), dtype=jnp.float32)
        gamma = jnp.ones((dim,), dtype=jnp.float32)
        w_qkv = jax.random.normal(k2, (dim, 3 * dim_inner), dtype=jnp.float32) * dim ** (-0.5)
        w_out = jax.random.normal(k3, (dim_inner, dim), dtype=jnp.float32) * dim_inner ** (-0.5)
        return {'x': x, 'gamma': gamma, 'w_qkv': w_qkv, 'w_out': w_out}
    _L0_attn_in = _L0_attn_setup()

    def _L0_ffn_setup():
        import jax, jax.numpy as jnp
        import numpy as np
        B, S, D, F, E = (2, 256, 128, 512, 8)
        LN_EPS = 1e-05

        def _layer_norm(x, gamma, beta):
            mu = jnp.mean(x, axis=-1, keepdims=True)
            var = jnp.mean(jnp.square(x - mu), axis=-1, keepdims=True)
            return (x - mu) * jax.lax.rsqrt(var + LN_EPS) * gamma + beta
        key = jax.random.key(seed)
        ks = jax.random.split(key, 8)

        def xavier(k, shape):
            fan_in, fan_out = (shape[-1], shape[-2])
            a = jnp.sqrt(6.0 / (fan_in + fan_out))
            return jax.random.uniform(k, shape, jnp.float32, -a, a)
        return {'tgt': jax.random.normal(ks[0], (B, S, D), jnp.float32), 'Wr': xavier(ks[1], (E, D)), 'br': jnp.zeros((E,), jnp.float32), 'W1': xavier(ks[2], (E, F, D)), 'b1': jnp.zeros((E, F), jnp.float32), 'W2': xavier(ks[3], (E, D, F)), 'b2': jnp.zeros((E, D), jnp.float32), 'gamma': jnp.ones((D,), jnp.float32), 'beta': jnp.zeros((D,), jnp.float32)}
    _L0_ffn_in = _L0_ffn_setup()
    _d = {'L0_attn_x': _L0_attn_in['x'], 'L0_attn_gamma': _L0_attn_in['gamma'], 'L0_attn_w_qkv': _L0_attn_in['w_qkv'], 'L0_attn_w_out': _L0_attn_in['w_out'], 'L0_ffn_Wr': _L0_ffn_in['Wr'], 'L0_ffn_br': _L0_ffn_in['br'], 'L0_ffn_W1': _L0_ffn_in['W1'], 'L0_ffn_b1': _L0_ffn_in['b1'], 'L0_ffn_W2': _L0_ffn_in['W2'], 'L0_ffn_b2': _L0_ffn_in['b2'], 'L0_ffn_gamma': _L0_ffn_in['gamma'], 'L0_ffn_beta': _L0_ffn_in['beta']}
    _x0 = _d['L0_attn_x']
    _d['L0_attn_x'] = jax.random.normal(jax.random.fold_in(jax.random.key(seed), 1), (4, 1024, 128), dtype=_x0.dtype)
    del _x0
    return _d

def reference(L0_attn_x, L0_attn_gamma, L0_attn_w_qkv, L0_attn_w_out, L0_ffn_Wr, L0_ffn_br, L0_ffn_W1, L0_ffn_b1, L0_ffn_W2, L0_ffn_b2, L0_ffn_gamma, L0_ffn_beta):

    def _L0_attn_ref(x, gamma, w_qkv, w_out):
        import jax, jax.numpy as jnp
        import numpy as np
        HEADS = 16
        DIM_HEAD = 64
        RMS_EPS = 1e-12
        b, n, dim = x.shape
        h, d = (HEADS, DIM_HEAD)
        l2 = jnp.maximum(jnp.linalg.norm(x, axis=-1, keepdims=True), RMS_EPS)
        normed = x / l2 * dim ** 0.5 * gamma
        qkv = (normed @ w_qkv).reshape(b, n, 3, h, d)
        qkv = jnp.transpose(qkv, (2, 0, 3, 1, 4))
        q, k, v = (qkv[0], qkv[1], qkv[2])
        q = q * d ** (-0.5)
        sim = jnp.einsum('bhid,bhjd->bhij', q, k)
        mask_value = -jnp.finfo(sim.dtype).max
        causal_mask = jnp.triu(jnp.ones((n, n), dtype=bool), k=1)
        sim = jnp.where(causal_mask, mask_value, sim)
        attn = jax.nn.softmax(sim, axis=-1)
        out = jnp.einsum('bhij,bhjd->bhid', attn, v)
        out = jnp.transpose(out, (0, 2, 1, 3)).reshape(b, n, h * d)
        return out @ w_out

    def _L0_ffn_ref(tgt, Wr, br, W1, b1, W2, b2, gamma, beta):
        import jax, jax.numpy as jnp
        import numpy as np
        B, S, D, F, E = (2, 256, 128, 512, 8)
        LN_EPS = 1e-05

        def _layer_norm(x, gamma, beta):
            mu = jnp.mean(x, axis=-1, keepdims=True)
            var = jnp.mean(jnp.square(x - mu), axis=-1, keepdims=True)
            return (x - mu) * jax.lax.rsqrt(var + LN_EPS) * gamma + beta
        logits = jnp.einsum('bsd,ed->bse', tgt, Wr) + br
        top_v, top_i = jax.lax.top_k(logits, 2)
        top_w = jax.nn.softmax(top_v, axis=-1)
        n_exp = logits.shape[-1]
        router_w = jnp.sum(jax.nn.one_hot(top_i, n_exp, dtype=top_w.dtype) * top_w[..., None], axis=-2)
        h = jnp.einsum('bsd,efd->bsef', tgt, W1) + b1
        h = jax.nn.relu(h)
        o = jnp.einsum('bsef,edf->bsed', h, W2) + b2
        tgt2 = jnp.einsum('bsed,bse->bsd', o, router_w)
        return _layer_norm(tgt + tgt2, gamma, beta)
    x = L0_attn_x
    xn = _layernorm(x, axis=-1)
    x = x + _L0_attn_ref(xn, L0_attn_gamma, L0_attn_w_qkv, L0_attn_w_out) + _L0_ffn_ref(xn, L0_ffn_Wr, L0_ffn_br, L0_ffn_W1, L0_ffn_b1, L0_ffn_W2, L0_ffn_b2, L0_ffn_gamma, L0_ffn_beta)
    return x

_drawn_inputs = setup_inputs


def setup_inputs(seed=0):
    import zlib

    import numpy as np

    out = dict(_drawn_inputs(seed))
    spreads = {'L0_attn_gamma': (1.0, 0.2),
     'L0_ffn_br': (0.0, 0.1),
     'L0_ffn_b1': (0.0, 0.1),
     'L0_ffn_b2': (0.0, 0.1),
     'L0_ffn_gamma': (1.0, 0.2),
     'L0_ffn_beta': (0.0, 0.1)}
    factors = {}
    for name, (base, spread) in spreads.items():
        noise = np.random.default_rng([zlib.crc32(name.encode()), seed]).standard_normal(out[name].shape)
        drawn = base * np.exp(spread * noise) if base else spread * noise
        out[name] = jnp.asarray(drawn.astype(out[name].dtype))
    for name, factor in factors.items():
        out[name] = (out[name] * factor).astype(out[name].dtype)
    return out
```

```python
from contextlib import ExitStack

import concourse.bass as bass
from concourse import mybir

ALU = mybir.AluOpType
ACT = mybir.ActivationFunctionType
AX_X = mybir.AxisListType.X
F32 = mybir.dt.float32
F32R = mybir.dt.float32r
BF16 = mybir.dt.bfloat16

P = 128
BANK = 512
LN_EPS = 1e-5
RMS_EPS = 1e-12
TINY = 1e-30
MASKED = -1e30


def attention_and_experts(nc, x, attn_gamma, w_qkv, w_out, w_router, b_router,
                          w1, b1, w2, b2, ffn_gamma, ffn_beta, out):
    BATCH, SEQ, D = x.shape
    EXPERTS, FF, _ = w1.shape
    HEAD = 64
    HEADS = w_out.shape[0] // HEAD
    PAIRS = HEADS // 2
    TILES = SEQ // P
    ALL_TILES = BATCH * TILES
    HALVES = SEQ // BANK
    GROUP = BANK // P
    GROUPS = ALL_TILES // GROUP
    FT = FF // P
    SCALE = float(HEAD) ** -0.5
    assert D == P and SEQ == 2 * BANK and FF == BANK and 2 * HEAD == P

    x_tiles = x.rearrange("b (t p) d -> p (b t) d", p=P)
    out_tiles = out.rearrange("b (t p) d -> p (b t) d", p=P)

    with ExitStack() as whole:
        def sb(ctx, name, shape, dt=F32):
            return ctx.enter_context(nc.sbuf_tensor(name, shape, dt))

        def ps(ctx, name, shape, dt=F32):
            return ctx.enter_context(nc.psum_tensor(name, shape, dt))

        def sem(name):
            return whole.enter_context(nc.semaphore(name))

        acc = sb(whole, "acc", [P, ALL_TILES, D])
        nT = sb(whole, "nT", [P, ALL_TILES * P])
        nT_hi = sb(whole, "nT_hi", [P, ALL_TILES * P], F32R)
        nT_lo = sb(whole, "nT_lo", [P, ALL_TILES * P], F32R)
        ident = sb(whole, "ident", [P, P])

        x_loaded = [sem(f"x_loaded{i}") for i in range(BATCH)]
        w1_loaded = sem("w1_loaded")
        w2_loaded = sem("w2_loaded")
        small_loaded = sem("small_loaded")
        ident_zeroed = sem("ident_zeroed")
        consts_ready = sem("consts_ready")
        dve_step = sem("dve_step")
        sqrt_asked = sem("sqrt_asked")
        sqrt_done = sem("sqrt_done")
        normed_ready = sem("normed_ready")
        waited = sem("waited")
        turned = sem("turned")
        split_hi = sem("split_hi")
        bank_free = [sem(f"bank_free{i}") for i in range(4)]
        nT_hi_done = sem("nT_hi_done")
        xnT_done = sem("xnT_done")
        experts_ready = sem("experts_ready")
        router_ready = sem("router_ready")
        logits_done = sem("logits_done")
        shifted = sem("shifted")
        exp_router = sem("exp_router")
        weights_ready = sem("weights_ready")
        rwT_turned = sem("rwT_turned")
        rwT_copied = sem("rwT_copied")
        b2_done = sem("b2_done")
        b2_added = sem("b2_added")
        hidden_done = sem("hidden_done")
        relu_done = sem("relu_done")
        expert_out = sem("expert_out")
        expert_added = sem("expert_added")
        x_again = sem("x_again")
        ln_sqrt_asked = sem("ln_sqrt_asked")
        ln_sqrt_done = sem("ln_sqrt_done")
        ffn_done = sem("ffn_done")

        with ExitStack() as ph1:
            xs = sb(ph1, "xs", [P, 2, TILES, D])
            nrm = sb(ph1, "nrm", [P, 2, TILES, D])
            w1_raw = sb(ph1, "w1_raw", [P, EXPERTS * FT, D])
            w2_raw = sb(ph1, "w2_raw", [P, EXPERTS, FF])
            hT = w1_raw[:].rearrange("p (i f q) d -> p i f (q d)", i=2, f=FT)
            rank = w1_raw[:].rearrange("p (i s) d -> p i (s d)", i=2)
            w1T_hi = sb(ph1, "w1T_hi", [P, EXPERTS, FF], F32R)
            w1T_lo = sb(ph1, "w1T_lo", [P, EXPERTS, FF], F32R)
            w2T = sb(ph1, "w2T", [P, EXPERTS, FT, D])
            xnT_hi = sb(ph1, "xnT_hi", [P, ALL_TILES * P], F32R)
            xnT_lo = sb(ph1, "xnT_lo", [P, ALL_TILES * P], F32R)
            wr_raw = sb(ph1, "wr_raw", [EXPERTS, D])
            b1_raw = sb(ph1, "b1_raw", [EXPERTS * FT, P])
            b2_sb = sb(ph1, "b2_sb", [EXPERTS, D])
            wrT_hi = sb(ph1, "wrT_hi", [P, EXPERTS], F32R)
            wrT_lo = sb(ph1, "wrT_lo", [P, EXPERTS], F32R)
            b1T = sb(ph1, "b1T", [P, EXPERTS * FT])
            br_all = sb(ph1, "br_all", [P, EXPERTS])
            agamma = sb(ph1, "agamma", [P, 1])
            fgamma = sb(ph1, "fgamma", [P, D])
            fbeta = sb(ph1, "fbeta", [P, D])
            before = sb(ph1, "before", [P, EXPERTS, EXPERTS])
            st = sb(ph1, "st", [P, 8, 2, TILES])
            ls = sb(ph1, "ls", [P, 8, GROUP])
            logit = sb(ph1, "logit", [P, ALL_TILES, EXPERTS])
            chosen = sb(ph1, "chosen", [P, ALL_TILES, EXPERTS])
            route = sb(ph1, "route", [P, ALL_TILES, EXPERTS])
            top = sb(ph1, "top", [P, ALL_TILES])
            wsum = sb(ph1, "wsum", [P, ALL_TILES])
            rwT = sb(ph1, "rwT", [EXPERTS, 2, BANK])
            bank = [ps(ph1, f"bank{i}", [P, BANK]) for i in range(4)]
            obank = [ps(ph1, f"obank{i}", [P, GROUP, D]) for i in range(2)]
            lbank = ps(ph1, "lbank", [P, ALL_TILES, EXPERTS])
            tbank = ps(ph1, "tbank", [P, BANK])

            units = [("w1", e) for e in range(EXPERTS)] + [("w2", e) for e in range(EXPERTS)]
            units += [("wr", 0), ("b1", 0)]
            for g in range(GROUPS):
                units += [("xn", g), ("n", g)]
            n_hi = {}
            for u, (kind, _) in enumerate(units):
                if kind in ("w1", "wr", "xn"):
                    n_hi[u] = len(n_hi) + 1

            with nc.Block() as block:

                @block.sync
                def _(sp):
                    for b in range(BATCH):
                        if b >= 2:
                            sp.wait_ge(normed_ready, b - 1)
                        sp.dma_start(xs[:, b % 2], x_tiles[:, b * TILES:(b + 1) * TILES]).then_inc(x_loaded[b], 16)
                    sp.wait_ge(normed_ready, BATCH)
                    with sp.Fori(0, GROUPS) as g:
                        sp.wait_ge(ffn_done, g + 1)
                        sp.dma_start(xs[:, 0, 0:GROUP], x_tiles[:, bass.ds(g * GROUP, GROUP)]).then_inc(x_again, 16)

                @block.gpsimd
                def _(pool):
                    pool.memset(ident[:], 1.0).then_inc(ident_zeroed, 1)
                    pool.memset(before[:], 1.0).then_inc(ident_zeroed, 1)
                    pool.wait_ge(ident_zeroed, 2)
                    pool.affine_select(out=ident[:], in_=ident[:], pattern=[[1, P]], compare_op=ALU.is_equal,
                                       fill=0.0, base=0, channel_multiplier=-1).then_inc(consts_ready, 1)
                    pool.affine_select(out=before[:], in_=before[:], pattern=[[1, EXPERTS], [-1, EXPERTS]],
                                       compare_op=ALU.is_gt, fill=0.0, base=0,
                                       channel_multiplier=0).then_inc(consts_ready, 1)

                @block.scalar
                def _(act):
                    act.dma_start(w1_raw[:], w1.rearrange("e (f p) d -> p (e f) d", p=P)).then_inc(w1_loaded, 16)
                    act.dma_start(w2_raw[:], w2.rearrange("e d f -> d e f")).then_inc(w2_loaded, 16)
                    with nc.allow_non_contiguous_dma(reason="one column of gamma"):
                        act.dma_start(agamma[:], attn_gamma.rearrange("(p a) -> p a", a=1)).then_inc(small_loaded, 16)
                    act.dma_start(wr_raw[:], w_router).then_inc(small_loaded, 16)
                    act.dma_start(b1_raw[:], b1.rearrange("e (f p) -> (e f) p", p=P)).then_inc(small_loaded, 16)
                    act.dma_start(b2_sb[:], b2).then_inc(small_loaded, 16)
                    act.dma_start(br_all[:], b_router.partition_broadcast(P)).then_inc(small_loaded, 16)
                    act.dma_start(fgamma[:], ffn_gamma.partition_broadcast(P)).then_inc(small_loaded, 16)
                    act.dma_start(fbeta[:], ffn_beta.partition_broadcast(P)).then_inc(small_loaded, 16)

                    def roots(b):
                        act.wait_ge(sqrt_asked, b + 1)
                        act.activation(st[:, 3], st[:, 2], ACT.Sqrt).then_inc(sqrt_done, 1)

                    def evacuate(u):
                        kind, n = units[u]
                        src = bank[u % 4]
                        if kind == "n":
                            act.wait_ge(bank_free[u % 4], u // 4 + 1)
                            cols = slice(n * BANK, (n + 1) * BANK)
                            act.activation(nT_hi[:, cols], nT[:, cols], ACT.Copy).then_inc(nT_hi_done, 1)
                            return
                        act.wait_ge(turned, u + 1)
                        if kind == "w1":
                            act.activation(w1T_hi[:, n], src[:], ACT.Copy).then_inc(split_hi, 1)
                        elif kind == "wr":
                            act.activation(wrT_hi[:], src[:, 0:EXPERTS], ACT.Copy).then_inc(split_hi, 1)
                        elif kind == "xn":
                            act.activation(xnT_hi[:, n * BANK:(n + 1) * BANK], src[:], ACT.Copy).then_inc(split_hi, 1)
                        elif kind == "w2":
                            act.activation(w2T[:, n].rearrange("p f d -> p (f d)"), src[:],
                                           ACT.Copy).then_inc(bank_free[u % 4], 1)
                        elif kind == "b1":
                            act.activation(b1T[:], src[:, 0:EXPERTS * FT], ACT.Copy).then_inc(bank_free[u % 4], 1)

                    first_x = units.index(("xn", 0))
                    for u in range(first_x):
                        evacuate(u)
                        if u in (3, 7):
                            roots(u // 4)
                    per_batch = 2 * TILES // GROUP
                    for b in range(BATCH):
                        for u in range(first_x + b * per_batch, first_x + (b + 1) * per_batch):
                            evacuate(u)
                        if b + 2 < BATCH:
                            roots(b + 2)

                    act.wait_ge(shifted, 1)
                    act.activation(route[:], logit[:], ACT.Exp).then_inc(exp_router, 1)
                    for g in range(GROUPS):
                        act.wait_ge(rwT_turned, g + 1)
                        if g >= 2:
                            act.wait_ge(b2_done, g - 1)
                        act.activation(rwT[:, g % 2], tbank[0:EXPERTS, :], ACT.Copy).then_inc(rwT_copied, 1)

                    with act.Fori(0, GROUPS) as g:
                        for e in range(EXPERTS):
                            for f in range(FT):
                                act.wait_ge(hidden_done, g * (EXPERTS * FT) + (e * FT + f + 1))
                                act.activation(hT[:, e % 2, f], bank[f][:], ACT.Relu,
                                               bias=b1T[:, e * FT + f:e * FT + f + 1]).then_inc(relu_done, 1)
                        act.wait_ge(ln_sqrt_asked, g + 1)
                        act.activation(ls[:, 3], ls[:, 2], ACT.Sqrt).then_inc(ln_sqrt_done, 1)

                @block.vector
                def _(dve):
                    steps = [0]

                    def then(ins):
                        steps[0] += 1
                        ins.then_inc(dve_step, 1)
                        dve.wait_ge(dve_step, steps[0])

                    def over_features(small, tiles):
                        return small.unsqueeze(2).broadcast_to([P, tiles, D])

                    def layernorm(b):
                        xb, ab, nb = xs[:, b % 2], acc[:, b * TILES:(b + 1) * TILES], nrm[:, b % 2]
                        dve.wait_ge(x_loaded[b], 16)
                        if b >= 2:
                            dve.wait_ge(turned, units.index(("n", (b - 1) * TILES // GROUP - 1)) + 1)
                        then(dve.tensor_reduce(st[:, 0, 0], xb, AX_X, ALU.add))
                        then(dve.tensor_scalar(st[:, 0, 1], st[:, 0, 0], 1.0 / D, None, ALU.mult))
                        then(dve.tensor_tensor(ab, xb, over_features(st[:, 0, 1], TILES), ALU.subtract))
                        then(dve.tensor_tensor(nb, ab, ab, ALU.mult))
                        then(dve.tensor_reduce(st[:, 1, 0], nb, AX_X, ALU.add))
                        dve.tensor_scalar(st[:, 2, 0], st[:, 1, 0], 1.0 / D, LN_EPS, ALU.mult, ALU.add)
                        dve.tensor_scalar(st[:, 2, 1], st[:, 1, 0], TINY, None, ALU.max).then_inc(sqrt_asked, 1)
                        dve.wait_ge(sqrt_asked, b + 1)
                        dve.wait_ge(sqrt_done, b + 1)
                        then(dve.reciprocal(st[:, 4], st[:, 3]))
                        then(dve.tensor_tensor(st[:, 4], st[:, 4], st[:, 2], ALU.mult))
                        then(dve.tensor_tensor(st[:, 4], st[:, 4], st[:, 3], ALU.add))
                        then(dve.tensor_scalar(st[:, 4], st[:, 4], 0.5, None, ALU.mult))
                        then(dve.reciprocal(st[:, 5, 0], st[:, 4, 0]))
                        then(dve.tensor_tensor(st[:, 6, 0], st[:, 4, 1], st[:, 5, 0], ALU.mult))
                        then(dve.tensor_scalar(st[:, 6, 0], st[:, 6, 0], RMS_EPS, None, ALU.max))
                        then(dve.reciprocal(st[:, 6, 1], st[:, 6, 0]))
                        then(dve.tensor_scalar(st[:, 6, 1], st[:, 6, 1], float(D) ** 0.5, None, ALU.mult))
                        then(dve.tensor_tensor(ab, ab, over_features(st[:, 5, 0], TILES), ALU.mult))
                        dve.tensor_tensor(nb, ab, over_features(st[:, 6, 1], TILES),
                                          ALU.mult).then_inc(normed_ready, 1)

                    def evacuate(u):
                        kind, n = units[u]
                        src = bank[u % 4]
                        if kind in ("w2", "b1"):
                            return
                        if kind == "n":
                            dve.wait_ge(turned, u + 1)
                            cols = slice(n * BANK, (n + 1) * BANK)
                            dve.tensor_scalar(nT[:, cols], src[:], agamma[:, 0:1], None,
                                              ALU.mult).then_inc(bank_free[u % 4], 1)
                            if n:
                                lower_half_of_n(n - 1)
                            return
                        dve.wait_ge(split_hi, n_hi[u])
                        if kind == "w1":
                            dve.tensor_tensor(w1T_lo[:, n], src[:], w1T_hi[:, n].bitcast(F32),
                                              ALU.subtract).then_inc(bank_free[u % 4], 1)
                        elif kind == "wr":
                            dve.tensor_tensor(wrT_lo[:], src[:, 0:EXPERTS], wrT_hi[:].bitcast(F32),
                                              ALU.subtract).then_inc(bank_free[u % 4], 1)
                        elif kind == "xn":
                            cols = slice(n * BANK, (n + 1) * BANK)
                            dve.tensor_tensor(xnT_lo[:, cols], src[:], xnT_hi[:, cols].bitcast(F32),
                                              ALU.subtract).then_inc(bank_free[u % 4], 1)

                    def lower_half_of_n(n):
                        cols = slice(n * BANK, (n + 1) * BANK)
                        dve.wait_ge(nT_hi_done, n + 1)
                        dve.tensor_tensor(nT_lo[:, cols], nT[:, cols], nT_hi[:, cols].bitcast(F32), ALU.subtract)

                    first_x = units.index(("xn", 0))
                    for b in range(BATCH):
                        if b < 2:
                            layernorm(b)
                        for u in range(4 * b, 4 * b + 4):
                            evacuate(u)
                    dve.wait_ge(small_loaded, 16 * 7)
                    for u in range(4 * BATCH, first_x):
                        evacuate(u)
                    per_batch = 2 * TILES // GROUP
                    for b in range(BATCH):
                        for u in range(first_x + b * per_batch, first_x + (b + 1) * per_batch):
                            evacuate(u)
                        if b + 2 < BATCH:
                            layernorm(b + 2)
                    lower_half_of_n(GROUPS - 1)

                    dve.wait_ge(logits_done, 1)
                    then(dve.tensor_tensor(logit[:], lbank[:], br_all[:].unsqueeze(1).broadcast_to(
                        [P, ALL_TILES, EXPERTS]), ALU.add))
                    shape4 = [P, ALL_TILES, EXPERTS, EXPERTS]
                    mine = logit[:].unsqueeze(3).broadcast_to(shape4)
                    other = logit[:].unsqueeze(2).broadcast_to(shape4)
                    more = rank[:, 0].rearrange("p (t e f) -> p t e f", e=EXPERTS, f=EXPERTS)
                    same = rank[:, 1].rearrange("p (t e f) -> p t e f", e=EXPERTS, f=EXPERTS)
                    dve.wait_ge(consts_ready, 2)
                    dve.tensor_tensor(more, other, mine, ALU.is_gt)
                    then(dve.tensor_tensor(same, other, mine, ALU.is_equal))
                    then(dve.tensor_tensor(same, same, before[:].unsqueeze(1).broadcast_to(shape4), ALU.mult))
                    then(dve.tensor_tensor(more, more, same, ALU.add))
                    then(dve.tensor_reduce(chosen[:], more, AX_X, ALU.add))
                    then(dve.tensor_scalar(chosen[:], chosen[:], 1.5, None, ALU.is_lt))
                    then(dve.tensor_reduce(top[:], logit[:], AX_X, ALU.max))
                    over_experts = [P, ALL_TILES, EXPERTS]
                    dve.tensor_tensor(logit[:], logit[:], top[:].unsqueeze(2).broadcast_to(over_experts),
                                      ALU.subtract).then_inc(shifted, 1)
                    dve.wait_ge(exp_router, 1)
                    then(dve.tensor_tensor(route[:], route[:], chosen[:], ALU.mult))
                    then(dve.tensor_reduce(wsum[:], route[:], AX_X, ALU.add))
                    then(dve.reciprocal(wsum[:], wsum[:]))
                    dve.tensor_tensor(route[:], route[:], wsum[:].unsqueeze(2).broadcast_to(over_experts),
                                      ALU.mult).then_inc(weights_ready, 1)
                    for g in range(GROUPS):
                        dve.wait_ge(b2_done, g + 1)
                        dve.tensor_tensor(acc[:, g * GROUP:(g + 1) * GROUP], obank[g % 2][:],
                                          acc[:, g * GROUP:(g + 1) * GROUP], ALU.add).then_inc(b2_added, 1)
                    dve.wait_ge(b2_added, GROUPS)

                    dve.sem_inc(expert_added, 1)
                    dve.sem_inc(ffn_done, 1)
                    in_loop = steps[0]
                    PER = 13
                    with dve.Fori(0, GROUPS) as g:
                        ag = acc[:, bass.ds(g * GROUP, GROUP)]
                        for e in range(EXPERTS):
                            dve.wait_ge(expert_out, g * EXPERTS + (e + 1))
                            if e:
                                dve.wait_ge(expert_added, g * EXPERTS + (e + 1))
                            for q in range(GROUP):
                                tile = acc[:, bass.ds(g * GROUP + q, 1)].rearrange("p a d -> p (a d)")
                                weight = route[:, bass.ds(g * GROUP + q, 1), e:e + 1].rearrange("p a e -> p (a e)")
                                ins = dve.scalar_tensor_tensor(out=tile, in0=obank[e % 2][:, q], scalar=weight,
                                                               in1=tile, op0=ALU.mult, op1=ALU.add)
                            ins.then_inc(expert_added, 1)
                        dve.wait_ge(expert_added, g * EXPERTS + (EXPERTS + 1))
                        dve.sem_inc(waited, 1)
                        n = [0]

                        def then_g(ins):
                            n[0] += 1
                            ins.then_inc(dve_step, 1)
                            dve.wait_ge(dve_step, g * PER + (in_loop + n[0]))

                        ng = nrm[:, 0, 0:GROUP]
                        then_g(dve.tensor_reduce(ls[:, 0], ag, AX_X, ALU.add))
                        then_g(dve.tensor_scalar(ls[:, 0], ls[:, 0], 1.0 / D, None, ALU.mult))
                        then_g(dve.tensor_tensor(ag, ag, over_features(ls[:, 0], GROUP), ALU.subtract))
                        then_g(dve.tensor_tensor(ng, ag, ag, ALU.mult))
                        then_g(dve.tensor_reduce(ls[:, 1], ng, AX_X, ALU.add))
                        dve.tensor_scalar(ls[:, 2], ls[:, 1], 1.0 / D, LN_EPS, ALU.mult,
                                          ALU.add).then_inc(ln_sqrt_asked, 1)
                        dve.wait_ge(ln_sqrt_done, g + 1)
                        then_g(dve.reciprocal(ls[:, 4], ls[:, 3]))
                        then_g(dve.tensor_tensor(ls[:, 4], ls[:, 4], ls[:, 2], ALU.mult))
                        then_g(dve.tensor_tensor(ls[:, 4], ls[:, 4], ls[:, 3], ALU.add))
                        then_g(dve.tensor_scalar(ls[:, 4], ls[:, 4], 0.5, None, ALU.mult))
                        then_g(dve.reciprocal(ls[:, 5], ls[:, 4]))
                        then_g(dve.tensor_tensor(ag, ag, over_features(ls[:, 5], GROUP), ALU.mult))
                        then_g(dve.tensor_tensor(ag, ag, fgamma[:].unsqueeze(1).broadcast_to([P, GROUP, D]), ALU.mult))
                        then_g(dve.tensor_tensor(ag, ag, fbeta[:].unsqueeze(1).broadcast_to([P, GROUP, D]), ALU.add))
                        assert n[0] == PER
                        dve.wait_ge(x_again, g * 16 + 16)
                        dve.tensor_tensor(ag, ag, xs[:, 0, 0:GROUP], ALU.add).then_inc(ffn_done, 1)

                @block.tensor
                def _(pe):
                    pe.wait_ge(consts_ready, 1)
                    pe.wait_ge(w1_loaded, 16)
                    for u, (kind, n) in enumerate(units):
                        if u >= 4:
                            pe.wait_ge(bank_free[u % 4], u // 4)
                        dst = bank[u % 4]
                        if kind == "w1":
                            for f in range(FT):
                                ins = pe.transpose(dst[:, f * P:(f + 1) * P], w1_raw[:, n * FT + f], ident[:])
                        elif kind == "w2":
                            if n == 0:
                                pe.wait_ge(w2_loaded, 16)
                            for f in range(FT):
                                ins = pe.transpose(dst[:, f * P:(f + 1) * P], w2_raw[:, n, f * P:(f + 1) * P],
                                                   ident[:])
                        elif kind == "wr":
                            pe.wait_ge(small_loaded, 16 * 7)
                            ins = pe.transpose(dst[:, 0:EXPERTS], wr_raw[:], ident[0:EXPERTS, 0:EXPERTS])
                        elif kind == "b1":
                            ins = pe.transpose(dst[:, 0:EXPERTS * FT], b1_raw[:],
                                               ident[0:EXPERTS * FT, 0:EXPERTS * FT])
                        else:
                            b = n * GROUP // TILES
                            pe.wait_ge(normed_ready, b + 1)
                            for q in range(GROUP):
                                t = n * GROUP + q
                                src = acc[:, t] if kind == "xn" else nrm[:, b % 2, t % TILES]
                                ins = pe.transpose(dst[:, q * P:(q + 1) * P], src, ident[:])
                        ins.then_inc(turned, 1)

                    for i in range(4):
                        pe.wait_ge(bank_free[i], len(range(i, len(units), 4)))
                    for t in range(ALL_TILES):
                        cols = slice(t * P, (t + 1) * P)
                        for n, (a, w) in enumerate(((xnT_hi, wrT_hi), (xnT_hi, wrT_lo), (xnT_lo, wrT_hi))):
                            ins = pe.matmul(lbank[:, t], a[:, cols], w[:], start=(n == 0), stop=(n == 2))
                    ins.then_inc(logits_done, 1)

                    pe.wait_ge(weights_ready, 1)
                    for g in range(GROUPS):
                        if g:
                            pe.wait_ge(rwT_copied, g)
                        for q in range(GROUP):
                            ins = pe.transpose(tbank[0:EXPERTS, q * P:(q + 1) * P], route[:, g * GROUP + q], ident[:])
                        ins.then_inc(rwT_turned, 1)
                        pe.wait_ge(rwT_copied, g + 1)
                        if g >= 2:
                            pe.wait_ge(b2_added, g - 1)
                        for q in range(GROUP):
                            ins = pe.matmul(obank[g % 2][:, q], rwT[:, g % 2, q * P:(q + 1) * P], b2_sb[:],
                                            start=True, stop=True)
                        ins.then_inc(b2_done, 1)
                    pe.wait_ge(b2_added, GROUPS)
                    pe.wait_ge(exp_router, 1)

                    with pe.Fori(0, GROUPS) as g:
                        toks = bass.ds(g * BANK, BANK)
                        for e in range(EXPERTS + 1):
                            for f in range(FT):
                                if e < EXPERTS:
                                    if e:
                                        pe.wait_ge(relu_done, g * (EXPERTS * FT) + ((e - 1) * FT + f + 1))
                                    rows = slice(f * P, (f + 1) * P)
                                    pe.matmul(bank[f][:], w1T_hi[:, e, rows], xnT_hi[:, toks], start=True, stop=False)
                                    pe.matmul(bank[f][:], w1T_hi[:, e, rows], xnT_lo[:, toks], start=False, stop=False)
                                    pe.matmul(bank[f][:], w1T_lo[:, e, rows], xnT_hi[:, toks], start=False,
                                              stop=True).then_inc(hidden_done, 1)
                                if e:
                                    o = e - 1
                                    q = f
                                    if q == 0:
                                        pe.wait_ge(relu_done, g * (EXPERTS * FT) + e * FT)
                                        if o >= 2:
                                            pe.wait_ge(expert_added, g * EXPERTS + (o - 1 + 1))
                                        elif o == 0:
                                            pe.wait_ge(expert_added, g * EXPERTS + 1)
                                    for k in range(FT):
                                        ins = pe.matmul(obank[o % 2][:, q], hT[:, o % 2, k, q * P:(q + 1) * P],
                                                        w2T[:, o, k], start=(k == 0), stop=(k == FT - 1))
                                    if q == GROUP - 1:
                                        ins.then_inc(expert_out, 1)

        qkv_loaded = sem("qkv_loaded")
        wout_loaded = sem("wout_loaded")
        wqk_hi_done = sem("wqk_hi_done")
        wqk_split = sem("wqk_split")
        mask_zeroed = sem("mask_zeroed")
        attn_consts = sem("attn_consts")
        max_scores = sem("max_scores")
        max_taken = sem("max_taken")
        max_split = sem("max_split")
        max_step = sem("max_step")
        misc_ready = sem("misc_ready")
        hi_done = sem("hi_done")
        lo_done = sem("lo_done")
        v_hi_done = sem("v_hi_done")
        v_done = sem("v_done")
        full_split = sem("full_split")
        diag_split = sem("diag_split")
        copies_done = sem("copies_done")
        shift_done = sem("shift_done")
        scores_ready = sem("scores_ready")
        probs_ready = sem("probs_ready")
        diag_masked = sem("diag_masked")
        pv_done = sem("pv_done")
        heads_out = [sem(f"heads_out{i}") for i in range(2)]
        recip_done = sem("recip_done")
        y_added = sem("y_added")
        stored = sem("stored")

        with ExitStack() as ph2:
            q_a = [[sb(ph2, f"q_a{i}{s}", [P, SEQ], F32R) for s in range(2)] for i in range(2)]
            k_a = [[sb(ph2, f"k_a{i}{s}", [P, SEQ], F32R) for s in range(2)] for i in range(2)]
            q_b = [[sb(ph2, f"q_b{i}{s}", [HEAD + 2, SEQ], F32R) for s in range(2)] for i in range(2)]
            k_b = [[sb(ph2, f"k_b{i}{s}", [HEAD + 2, SEQ], F32R) for s in range(2)] for i in range(2)]
            v_hi = [sb(ph2, f"v_hi{i}", [P, TILES, 2, HEAD + 1], F32R) for i in range(2)]
            v_lo = [sb(ph2, f"v_lo{i}", [P, TILES, 2, HEAD], F32R) for i in range(2)]
            RING = 4
            probs = sb(ph2, "probs", [P, RING, BANK])
            p_hi = sb(ph2, "p_hi", [P, RING, BANK], F32R)
            p_lo = sb(ph2, "p_lo", [P, RING, BANK], F32R)
            heads = sb(ph2, "heads", [HEAD + 1, 2, SEQ])
            w_raw = sb(ph2, "w_raw", [P, 3, P])
            wqk_hi = sb(ph2, "wqk_hi", [P, 2, P], F32R)
            wqk_lo = sb(ph2, "wqk_lo", [P, 2, P], F32R)
            wo = sb(ph2, "wo", [HEAD + 1, 2, D + 1])
            mask = sb(ph2, "mask", [P, SEQ])
            unread = sb(ph2, "unread", [P, 2, SEQ], BF16)
            row_max = sb(ph2, "row_max", [P, 2, TILES])
            shift = sb(ph2, "shift", [P, 2, TILES, 2], F32R)
            rden = sb(ph2, "rden", [P, 2, 4])
            max_ps = ps(ph2, "max_ps", [P, SEQ])
            score_ps = [ps(ph2, f"score_ps{i}", [P, BANK]) for i in range(2)]
            head_ps = ps(ph2, "head_ps", [P, SEQ])
            misc_ps = [ps(ph2, f"misc_ps{i}", [P, BANK]) for i in range(2)]

            chunks = [(half, j, max(half * BANK, j * P))
                      for half, keys in ((0, (0, 3, 1, 2)), (1, (0, 7, 1, 6, 2, 5, 4, 3))) for j in keys]
            LAST = [3, 11]
            CH = len(chunks)
            DIAG = [q0 == j * P for _, j, q0 in chunks]
            LAG = 3
            G = BATCH * 2
            MAX_AT = [1, 2, 3, 4, 5, 7, 9, 11]
            PROJECT_AT = [{0: 0, 1: 1, 3: 2, 5: 3}, {1: 4, 5: 5}]
            Y_AT = [4, 7, 9]
            y_units = [(0, 3), (3, 3), (6, 2)]

            def plan(last):
                order = []
                for g in range(G):
                    more = not (last and g == G - 1)
                    for c in range(CH):
                        order.append(("score", g, c))
                        if c >= LAG - 1:
                            order.append(("low", g, c - LAG + 1))
                        elif g:
                            order.append(("low", g - 1, CH + c - LAG + 1))
                        if more and c in MAX_AT:
                            order.append(("max", g + 1, MAX_AT.index(c)))
                        if c in PROJECT_AT[g % 2] and not (last and g >= G - 2):
                            order.append(("project", g // 2 + 1, PROJECT_AT[g % 2][c]))
                        if g and c in Y_AT:
                            order.append(("y", g - 1, Y_AT.index(c)))
                        if more and c == 8:
                            order.append(("shift", g + 1, 0))
                        if c == 2:
                            order.append(("shift", g, 1))
                        if g == G - 3 and c == 10 and not last:
                            order.append(("weights", 0, 0))
                        if c >= LAG:
                            order.append(("pv", g, c - LAG))
                        elif g:
                            order.append(("pv", g - 1, CH + c - LAG))
                for c in range(CH - LAG, CH):
                    if c > CH - LAG:
                        order.append(("low", G - 1, c))
                    order.append(("pv", G - 1, c))
                for n in range(len(y_units)):
                    order.append(("y", G - 1, n))
                return numbered(order)

            def numbered(order):
                n, out_ = 0, []
                for o in order:
                    misc = o[0] in ("project", "shift", "y")
                    out_.append((*o, n if misc else None))
                    n += misc
                return out_

            first = numbered([("project", 0, n) for n in range(6)]
                             + [("max", 0, t) for t in range(TILES)] + [("shift", 0, 0)])
            MISC0 = sum(o[-1] is not None for o in first)
            MISC = sum(o[-1] is not None for o in plan(False))
            assert MISC % 2 == 0
            first_units = [o[:3] for o in first if o[-1] is not None]

            def n_max(hp, g, t):
                return hp * (G * TILES) + (g * TILES + t)

            def n_chunk(hp, g, c):
                return hp * (G * CH) + (g * CH + c)

            def n_diag(hp, g, c):
                return hp * (G * sum(DIAG)) + (g * sum(DIAG) + sum(DIAG[:c]))

            def n_full(hp, g, c):
                return hp * (G * (CH - sum(DIAG))) + (g * (CH - sum(DIAG)) + c - sum(DIAG[:c]))

            def n_misc(hp, u, start):
                return (0 if start else MISC0) + hp * MISC + u

            def bank_of(u, start):
                return (u + MISC0) % 2 if start else u % 2

            def n_half(hp, g, half):
                return hp * (G * 2) + (g * 2 + half)

            def n_y(hp, g, n):
                return hp * (G * len(y_units)) + (g * len(y_units) + n)

            def n_batch(hp, p):
                return hp * BATCH + p

            def run(eng, walk):
                with eng.Fori(0, PAIRS - 1) as hp:
                    walk(hp, plan(False), False)
                walk(PAIRS - 1, plan(True), True)

            with nc.Block() as block:

                @block.sync
                def _(sp):
                    def weights(hp):
                        src = w_qkv.rearrange("d (s h c) -> d s h c", s=3, c=P)
                        sp.dma_start(w_raw[:], src[:, :, bass.ds(hp, 1)].rearrange("d s h c -> d (s h) c")
                                     ).then_inc(qkv_loaded, 16)

                    def out_weights(hp):
                        src = w_out.rearrange("(h s c) d -> c h s d", s=2, c=HEAD)
                        sp.dma_start(wo[0:HEAD, :, 0:D], src[:, bass.ds(hp, 1)].rearrange("c h s d -> c (h s) d")
                                     ).then_inc(wout_loaded, 16)

                    def copies(hp, p):
                        i = p % 2
                        sp.wait_ge(hi_done, n_batch(hp, p) * 8 + 8)
                        for s in range(2):
                            k_hi, q_hi = k_a[i][s][0:HEAD, :].bitcast(F32), q_a[i][s][0:HEAD, :].bitcast(F32)
                            sp.dma_start(k_a[i][s][HEAD:P, :].bitcast(F32), k_hi).then_inc(copies_done, 16)
                            sp.dma_start(q_b[i][s][0:HEAD, :].bitcast(F32), q_hi).then_inc(copies_done, 16)

                    weights(0)
                    sp.wait_ge(attn_consts, 2)
                    out_weights(0)
                    copies(0, 0)

                    def walk(hp, order, last):
                        for o in order:
                            if o[0] == "project" and o[2] == 3:
                                copies(hp, o[1])
                            if o[0] == "project" and o[1] == BATCH - 1 and o[2] == 5 and not last:
                                sp.wait_ge(misc_ready, n_misc(hp, o[3], False) + 1)
                                weights(hp + 1)
                        if not last:
                            sp.wait_ge(misc_ready, n_misc(hp, order[-1][3], False) + 1)
                            out_weights(hp + 1)
                        else:
                            for p in range(BATCH):
                                sp.wait_ge(y_added, n_y(hp, 2 * p + 1, len(y_units) - 1) + 2)
                                sp.dma_start(out_tiles[:, p * TILES:(p + 1) * TILES],
                                             acc[:, p * TILES:(p + 1) * TILES]).then_inc(stored, 16)
                            sp.wait_ge(stored, 16 * BATCH)

                    run(sp, walk)

                @block.gpsimd
                def _(pool):
                    pool.memset(wo[:], 0.0).then_inc(mask_zeroed, 1)
                    pool.memset(mask[:], 0.0).then_inc(mask_zeroed, 1)
                    for i in range(2):
                        pool.memset(v_hi[i][:, :, :, HEAD:HEAD + 1].bitcast(F32), 1.0).then_inc(mask_zeroed, 1)
                    pool.wait_ge(mask_zeroed, 4)
                    tri = mask[:, SEQ - P:SEQ]
                    pool.affine_select(out=tri, in_=tri, pattern=[[-1, P]], compare_op=ALU.is_ge, fill=MASKED,
                                       base=0, channel_multiplier=1).then_inc(attn_consts, 1)
                    pool.wait_ge(attn_consts, 1)
                    pool.memset(wo[HEAD:HEAD + 1, :, D:D + 1], 1.0).then_inc(attn_consts, 1)
                    n = 2
                    for i in range(2):
                        for s in range(2):
                            pool.wait_ge(attn_consts, n)
                            pool.memset(k_b[i][s][HEAD:HEAD + 2, :].bitcast(F32), 1.0).then_inc(attn_consts, 1)
                            n += 1
                    pool.wait_ge(attn_consts, n)

                    def walk(hp, order, last):
                        for o in order:
                            if o[0] != "score":
                                continue
                            _, g, c, _ = o
                            slot = (g * CH + c) % RING
                            pool.wait_ge(probs_ready, n_chunk(hp, g, c) + 1 + 2)
                            if DIAG[c]:
                                pool.sem_inc(waited, 1)
                                for tile in (probs[:, slot, 0:P], p_hi[:, slot, 0:P].bitcast(F32)):
                                    out_tile = p_hi[:, slot, 0:P] if tile.tensor.name == "p_hi" else tile
                                    ins = pool.affine_select(out=out_tile, in_=tile, pattern=[[1, P]],
                                                             compare_op=ALU.is_ge, fill=0.0, base=0,
                                                             channel_multiplier=-1)
                                ins.then_inc(diag_masked, 1)
                            else:
                                pool.tensor_tensor(p_lo[:, slot], probs[:, slot], p_hi[:, slot].bitcast(F32),
                                                   ALU.subtract).then_inc(full_split, 1)

                    run(pool, walk)

                @block.scalar
                def _(act):
                    act.sem_inc(probs_ready, 2)
                    act.sem_inc(heads_out[0], 1)
                    act.sem_inc(heads_out[1], 1)

                    def w_hi(hp):
                        act.wait_ge(qkv_loaded, hp * 16 + 16)
                        act.activation(wqk_hi[:], w_raw[:, 0:2], ACT.Copy).then_inc(wqk_hi_done, 1)

                    def project(hp, p, n, u, start):
                        i = p % 2
                        act.wait_ge(misc_ready, n_misc(hp, u, start) + 1)
                        src = misc_ps[bank_of(u, start)]
                        if n < 4:
                            dst, cols = (q_a, k_a)[n // 2][i], slice(n % 2 * BANK, (n % 2 + 1) * BANK)
                            for s in range(2):
                                act.activation(dst[s][0:HEAD, cols], src[s * HEAD:(s + 1) * HEAD, :],
                                               ACT.Copy).then_inc(hi_done, 1)
                        else:
                            t = (n - 4) * GROUP
                            act.activation(v_hi[i][:, t:t + GROUP, :, 0:HEAD],
                                           src[:].rearrange("p (t s c) -> p t s c", s=2, c=HEAD),
                                           ACT.Copy).then_inc(v_hi_done, 1)

                    def shifts(hp, g, half, u, start):
                        act.wait_ge(misc_ready, n_misc(hp, u, start) + 1)
                        dst = q_b[g // 2 % 2][g % 2]
                        act.activation(dst[HEAD:HEAD + 2, half * BANK:(half + 1) * BANK], misc_ps[bank_of(u, start)][0:2, :],
                                       ACT.Copy).then_inc(shift_done, 1)

                    w_hi(0)
                    for o in first:
                        if o[0] == "project":
                            project(0, o[1], o[2], o[3], True)
                        elif o[0] == "shift":
                            shifts(0, o[1], o[2], o[3], True)

                    def walk(hp, order, last):
                        for o in order:
                            kind, g, c, u = o
                            if kind == "score":
                                half, j, q0 = chunks[c]
                                width = (half + 1) * BANK - q0
                                act.wait_ge(scores_ready, n_chunk(hp, g, c) + 1)
                                act.wait_ge(pv_done, n_chunk(hp, g, c) + 1)
                                for p in (probs, p_hi):
                                    ins = act.activation(p[:, (g * CH + c) % RING, 0:width],
                                                         score_ps[(g * CH + c) % 2][:, 0:width], ACT.Exp,
                                                         scale=SCALE)
                                ins.then_inc(probs_ready, 1)
                            elif kind == "project":
                                project(hp, g, c, u, False)
                            elif kind == "weights":
                                w_hi(hp + 1)
                            elif kind == "shift":
                                shifts(hp, g, c, u, False)
                            elif kind == "pv" and c in LAST:
                                half = LAST.index(c)
                                cols = slice(half * BANK, (half + 1) * BANK)
                                act.wait_ge(pv_done, n_chunk(hp, g, c) + 1 + RING)
                                act.activation(heads[:, g % 2, cols], head_ps[0:HEAD + 1, cols],
                                               ACT.Copy).then_inc(heads_out[half], 1)

                    run(act, walk)

                @block.vector
                def _(dve):
                    def w_lo(hp):
                        dve.wait_ge(wqk_hi_done, hp + 1)
                        dve.tensor_tensor(wqk_lo[:], w_raw[:, 0:2], wqk_hi[:].bitcast(F32),
                                          ALU.subtract).then_inc(wqk_split, 1)

                    def project(hp, p, n, u, start):
                        i = p % 2
                        if n >= 4:
                            t = (n - 4) * GROUP
                            dve.wait_ge(v_hi_done, n_batch(hp, p) * 2 + (n - 3))
                            dve.tensor_tensor(v_lo[i][:, t:t + GROUP],
                                              misc_ps[bank_of(u, start)][:].rearrange("p (t s c) -> p t s c", s=2, c=HEAD),
                                              v_hi[i][:, t:t + GROUP, :, 0:HEAD].bitcast(F32),
                                              ALU.subtract).then_inc(v_done, 1)
                            return
                        cols = slice(n % 2 * BANK, (n % 2 + 1) * BANK)
                        src = misc_ps[bank_of(u, start)]
                        for s in range(2):
                            dve.wait_ge(hi_done, n_batch(hp, p) * 8 + (n * 2 + s + 1))
                            hi = (q_a, k_a)[n // 2][i][s][0:HEAD, cols].bitcast(F32)
                            lo = q_a[i][s][HEAD:P, cols] if n < 2 else k_b[i][s][0:HEAD, cols]
                            ins = dve.tensor_tensor(lo, src[s * HEAD:(s + 1) * HEAD, :], hi, ALU.subtract)
                        ins.then_inc(lo_done, 1)

                    def maximum(hp, g, t):
                        width = (t + 1) * P
                        src = max_ps[:, t % 2 * BANK:t % 2 * BANK + width] if t < 4 else max_ps[:, 0:width]
                        dve.wait_ge(max_scores, n_max(hp, g, t) + 1)
                        if g or t >= 2:
                            dve.wait_ge(max_taken, n_max(hp, g, t) - 1)
                        dve.sem_inc(waited, 1)
                        dve.tensor_tensor_reduce(out=unread[:, t % 2, 0:width], in0=src, in1=mask[:, SEQ - width:SEQ],
                                                 scale=1.0, scalar=MASKED, op0=ALU.add, op1=ALU.max,
                                                 accum_out=row_max[:, g % 2, t:t + 1]).then_inc(max_taken, 1)
                        if t % 4 == 3:
                            rows = slice(t - 3, t + 1)
                            dve.wait_ge(max_taken, n_max(hp, g, t) + 1)
                            dve.tensor_scalar(shift[:, g % 2, rows, 0], row_max[:, g % 2, rows], -1.0, None,
                                              ALU.mult).then_inc(max_step, 1)
                            dve.wait_ge(max_step, n_half(hp, g, t // 4) + 1)
                            dve.scalar_tensor_tensor(out=shift[:, g % 2, rows, 1], in0=row_max[:, g % 2, rows],
                                                     scalar=-1.0, in1=shift[:, g % 2, rows, 0].bitcast(F32),
                                                     op0=ALU.mult, op1=ALU.subtract).then_inc(max_split, 1)

                    def add_y(hp, g, n, u):
                        t0, tiles = y_units[n]
                        src = misc_ps[bank_of(u, False)][:, 0:tiles * (D + 1)].rearrange("p (t d) -> p t d", t=tiles)
                        dve.wait_ge(misc_ready, n_misc(hp, u, False) + 1)
                        dve.reciprocal(rden[:, u % 2, 0:tiles], src[:, :, D]).then_inc(recip_done, 1)
                        dve.wait_ge(recip_done, n_y(hp, g, n) + 1)
                        for t in range(tiles):
                            row = acc[:, g // 2 * TILES + t0 + t]
                            ins = dve.scalar_tensor_tensor(out=row, in0=src[:, t, 0:D], scalar=rden[:, u % 2, t:t + 1],
                                                           in1=row, op0=ALU.mult, op1=ALU.add)
                        ins.then_inc(y_added, 1)

                    dve.sem_inc(pv_done, RING)
                    dve.sem_inc(y_added, 1)
                    w_lo(0)
                    dve.wait_ge(attn_consts, 1)
                    for o in first:
                        if o[0] == "project":
                            project(0, o[1], o[2], o[3], True)
                        elif o[0] == "max":
                            maximum(0, o[1], o[2])

                    def walk(hp, order, last):
                        for o in order:
                            kind, g, c, u = o
                            if kind == "max":
                                maximum(hp, g, c)
                            elif kind == "project":
                                project(hp, g, c, u, False)
                            elif kind == "weights":
                                w_lo(hp + 1)
                            elif kind == "y":
                                add_y(hp, g, c, u)
                            elif kind == "low" and DIAG[c]:
                                half, j, q0 = chunks[c]
                                slot, width = (g * CH + c) % RING, (half + 1) * BANK - q0
                                dve.wait_ge(diag_masked, n_diag(hp, g, c) + 1)
                                dve.tensor_tensor(p_lo[:, slot, 0:width], probs[:, slot, 0:width],
                                                  p_hi[:, slot, 0:width].bitcast(F32),
                                                  ALU.subtract).then_inc(diag_split, 1)

                    run(dve, walk)

                @block.tensor
                def _(pe):
                    def misc_bank(hp, u, start):
                        units = first_units if start else body_units
                        if u < 2 and not start:
                            pe.wait_ge(y_added, n_y(hp, 0, 0) + 1)
                            pe.wait_ge(v_done, n_batch(hp, 0) * 2 + 2)
                            pe.wait_ge(shift_done, n_half(hp, 0, 0) + 1)
                        elif u >= 2:
                            kind, g, n = units[u - 2]
                            if kind == "project" and n < 4:
                                pe.wait_ge(lo_done, n_batch(hp, g) * 4 + (n + 1))
                            elif kind == "project":
                                pe.wait_ge(v_done, n_batch(hp, g) * 2 + (n - 3))
                            elif kind == "shift":
                                pe.wait_ge(shift_done, n_half(hp, g, n) + 1)
                            else:
                                pe.wait_ge(y_added, n_y(hp, g, n) + 2)
                        return misc_ps[bank_of(u, start)]

                    def project(hp, p, n, u, start):
                        toks = (p % BATCH) * SEQ
                        dst = misc_bank(hp, u, start)
                        if n < 4:
                            w = n // 2
                            cols = slice(toks + n % 2 * BANK, toks + (n % 2 + 1) * BANK)
                            if n == 0:
                                pe.wait_ge(wqk_split, hp + (p // BATCH + 1))
                            pe.matmul(dst[:], wqk_hi[:, w], nT_hi[:, cols], start=True, stop=False)
                            pe.matmul(dst[:], wqk_hi[:, w], nT_lo[:, cols], start=False, stop=False)
                            ins = pe.matmul(dst[:], wqk_lo[:, w], nT_hi[:, cols], start=False, stop=True)
                        else:
                            for q in range(GROUP):
                                t0 = toks + ((n - 4) * GROUP + q) * P
                                ins = pe.matmul(dst[:, q * P:(q + 1) * P], nT[:, t0:t0 + P], w_raw[:, 2],
                                                start=True, stop=True)
                        ins.then_inc(misc_ready, 1)

                    def max_scores_of(hp, g, t):
                        i, s = g // 2 % 2, g % 2
                        width = (t + 1) * P
                        if t == 0 and s == 0:
                            pe.wait_ge(copies_done, n_batch(hp, g // 2) * 64 + 64)
                            pe.wait_ge(lo_done, n_batch(hp, g // 2) * 4 + 4)
                        if t == 0:
                            pe.wait_ge(max_taken, n_max(hp, g, 0))
                        elif t >= 4:
                            pe.wait_ge(max_taken, n_max(hp, g, t))
                        elif t >= 2:
                            pe.wait_ge(max_taken, n_max(hp, g, t) - 1)
                        base = t % 2 * BANK if t < 4 else 0
                        for k0 in range(0, width, BANK):
                            k1 = min(k0 + BANK, width)
                            ins = pe.matmul(max_ps[:, base + k0:base + k1], q_a[i][s][:, t * P:(t + 1) * P],
                                            k_a[i][s][:, k0:k1], start=True, stop=True)
                        ins.then_inc(max_scores, 1)

                    def shifts(hp, g, half, u, start):
                        dst = misc_bank(hp, u, start)
                        pe.wait_ge(max_split, n_half(hp, g, half) + 1)
                        for q in range(GROUP):
                            ins = pe.transpose(dst[0:2, q * P:(q + 1) * P],
                                               shift[:, g % 2, half * GROUP + q, :].bitcast(F32), ident[:])
                        ins.then_inc(misc_ready, 1)

                    def score(hp, g, c):
                        half, j, q0 = chunks[c]
                        i, s = g // 2 % 2, g % 2
                        dst = score_ps[(g * CH + c) % 2][:, 0:(half + 1) * BANK - q0]
                        keys, qs = slice(j * P, (j + 1) * P), slice(q0, (half + 1) * BANK)
                        pe.wait_ge(probs_ready, n_chunk(hp, g, c) + 1)
                        if j == 0:
                            pe.wait_ge(shift_done, n_half(hp, g, half) + 1)
                        pe.matmul(dst, k_a[i][s][:, keys], q_a[i][s][:, qs], start=True, stop=False)
                        pe.matmul(dst, k_b[i][s][:, keys], q_b[i][s][:, qs], start=False,
                                  stop=True).then_inc(scores_ready, 1)

                    def values(hp, g, c):
                        half, j, q0 = chunks[c]
                        i, s = g // 2 % 2, g % 2
                        width = (half + 1) * BANK - q0
                        if DIAG[c]:
                            pe.wait_ge(diag_split, n_diag(hp, g, c) + 1)
                        else:
                            pe.wait_ge(full_split, n_full(hp, g, c) + 1)
                        if j == 0:
                            pe.wait_ge(heads_out[half], hp * G + (g + 1))
                        if c == 0:
                            pe.wait_ge(v_done, n_batch(hp, g // 2) * 2 + 2)
                        slot, cols = (g * CH + c) % RING, slice(q0, (half + 1) * BANK)
                        pe.matmul(head_ps[0:HEAD + 1, cols], v_hi[i][:, j, s], p_hi[:, slot, 0:width],
                                  start=(j == 0), stop=False)
                        pe.matmul(head_ps[0:HEAD, cols], v_lo[i][:, j, s], p_hi[:, slot, 0:width],
                                  start=False, stop=False)
                        pe.matmul(head_ps[0:HEAD + 1, cols], v_hi[i][:, j, s], p_lo[:, slot, 0:width],
                                  start=False, stop=c in LAST).then_inc(pv_done, 1)

                    def project_out(hp, g, n, u):
                        t0, tiles = y_units[n]
                        dst = misc_bank(hp, u, False)
                        if n == 0:
                            pe.wait_ge(heads_out[0], hp * G + (g + 2))
                            pe.wait_ge(heads_out[1], hp * G + (g + 2))
                            if g == 0:
                                pe.wait_ge(wout_loaded, hp * 16 + 16)
                        for t in range(tiles):
                            q0 = (t0 + t) * P
                            ins = pe.matmul(dst[:, t * (D + 1):(t + 1) * (D + 1)], heads[:, g % 2, q0:q0 + P],
                                            wo[:, g % 2], start=True, stop=True)
                        ins.then_inc(misc_ready, 1)

                    body_units = []
                    pe.wait_ge(attn_consts, 6)
                    for o in first:
                        if o[0] == "project":
                            project(0, o[1], o[2], o[3], True)
                        elif o[0] == "max":
                            max_scores_of(0, o[1], o[2])
                        else:
                            shifts(0, o[1], o[2], o[3], True)

                    def walk(hp, order, last):
                        body_units[:] = [o[:3] for o in order if o[-1] is not None]
                        for kind, g, c, u in order:
                            if kind == "score":
                                score(hp, g, c)
                            elif kind == "max":
                                max_scores_of(hp, g, c)
                            elif kind == "project":
                                project(hp, g, c, u, False)
                            elif kind == "shift":
                                shifts(hp, g, c, u, False)
                            elif kind == "pv":
                                values(hp, g, c)
                            elif kind == "y":
                                project_out(hp, g, c, u)

                    run(pe, walk)


_INS = ['L0_attn_x', 'L0_attn_gamma', 'L0_attn_w_qkv', 'L0_attn_w_out', 'L0_ffn_Wr', 'L0_ffn_br', 'L0_ffn_W1',
        'L0_ffn_b1', 'L0_ffn_W2', 'L0_ffn_b2', 'L0_ffn_gamma', 'L0_ffn_beta']
_OUTS = [((4, 1024, 128), 'float32')]


def kernel(**inputs):
    import numpy as _np
    import concourse.bacc as _bacc
    from concourse import mybir as _mybir
    from concourse.bass_utils import run_bass_kernel_spmd as _run

    nc = _bacc.Bacc("TRN2", target_bir_lowering=False, num_devices=1)
    arrays, args = {}, []
    for name in _INS:
        a = _np.ascontiguousarray(inputs[name])
        arrays[f"in_{name}_dram"] = a
        args.append(nc.dram_tensor(f"in_{name}_dram", a.shape, _mybir.dt.from_np(a.dtype), kind="ExternalInput").ap())
    for i, (shape, dtype) in enumerate(_OUTS):
        dt = _mybir.dt.from_np(_np.dtype(dtype))
        args.append(nc.dram_tensor(f"out_{i}_dram", shape, dt, kind="ExternalOutput").ap())
    attention_and_experts(nc, *args)
    r = _run(nc, [arrays], core_ids=[0])
    got = tuple(r.results[0][f"out_{i}_dram"] for i in range(len(_OUTS)))
    return got[0]
```

```python
from contextlib import ExitStack

import concourse.bass as bass
from concourse import mybir

ALU = mybir.AluOpType
ACT = mybir.ActivationFunctionType
AX_X = mybir.AxisListType.X
F32 = mybir.dt.float32
F32R = mybir.dt.float32r
BF16 = mybir.dt.bfloat16
I32 = mybir.dt.int32
U32 = mybir.dt.uint32

P = 128
BANK = 512
LN_EPS = 1e-5
RMS_EPS = 1e-12
TINY = 1e-30
MASKED = -1e30


def attention_and_experts(nc, x, attn_gamma, w_qkv, w_out, w_router, b_router,
                          w1, b1, w2, b2, ffn_gamma, ffn_beta, out):
    BATCH, SEQ, D = x.shape
    EXPERTS, FF, _ = w1.shape
    HEAD = 64
    HEADS = w_out.shape[0] // HEAD
    PAIRS = HEADS // 2
    TILES = SEQ // P
    ALL_TILES = BATCH * TILES
    HALVES = SEQ // BANK
    GROUP = BANK // P
    GROUPS = ALL_TILES // GROUP
    FT = FF // P
    SCALE = float(HEAD) ** -0.5
    assert D == P and SEQ == 2 * BANK and FF == BANK and 2 * HEAD == P

    x_tiles = x.rearrange("b (t p) d -> p (b t) d", p=P)
    out_tiles = out.rearrange("b (t p) d -> p (b t) d", p=P)

    with ExitStack() as whole:
        def sb(ctx, name, shape, dt=F32):
            return ctx.enter_context(nc.sbuf_tensor(name, shape, dt))

        def ps(ctx, name, shape, dt=F32):
            return ctx.enter_context(nc.psum_tensor(name, shape, dt))

        def sem(name):
            return whole.enter_context(nc.semaphore(name))

        acc = sb(whole, "acc", [P, ALL_TILES, D])
        nT = sb(whole, "nT", [P, ALL_TILES * P])
        nT_hi = sb(whole, "nT_hi", [P, ALL_TILES * P], F32R)
        nT_lo = sb(whole, "nT_lo", [P, ALL_TILES * P], F32R)
        ident = sb(whole, "ident", [P, P])

        mean = sb(whole, "mean", [P, ALL_TILES])
        rstd = sb(whole, "rstd", [P, ALL_TILES])
        slots = sb(whole, "slots", [P, 2, ALL_TILES], U32)
        weights = sb(whole, "weights", [P, 2, ALL_TILES])

        REGIONS = 2
        RT = ALL_TILES // REGIONS
        REGION = 2 * RT + EXPERTS - 1
        SORTED = REGIONS * REGION
        sorted_x = nc.dram_tensor("sorted_x", [SORTED * P, D], F32).ap()
        sorted_y = nc.dram_tensor("sorted_y", [SORTED * P, D], F32).ap()

        x_loaded = [sem(f"x_loaded{i}") for i in range(BATCH)]
        w1_loaded = [sem(f"w1_loaded{i}") for i in range(2)]
        w2_loaded = sem("w2_loaded")
        small_loaded = sem("small_loaded")
        set_up = sem("set_up")
        zeroed = sem("zeroed")
        dve_step = sem("dve_step")
        xn_ready = sem("xn_ready")
        nrm_ready = sem("nrm_ready")
        turned = sem("turned")
        act_read = sem("act_read")
        bank_free = [sem(f"bank_free{i}") for i in range(4)]
        logits_done = sem("logits_done")
        exp_asked = sem("exp_asked")
        exp_done = sem("exp_done")
        chosen_ready = sem("chosen_ready")
        counted = sem("counted")
        slots_ready = sem("slots_ready")
        scattered = [sem(f"scattered{i}") for i in range(REGIONS)]
        rows_loaded = [sem(f"rows_loaded{i}") for i in range(4)]
        rows_turned = sem("rows_turned")
        rows_hi = sem("rows_hi")
        rows_split = sem("rows_split")
        hidden_done = sem("hidden_done")
        hidden_copied = sem("hidden_copied")
        hidden_turned = sem("hidden_turned")
        relu_done = sem("relu_done")
        expert_out = sem("expert_out")
        expert_copied = sem("expert_copied")
        expert_stored = [sem(f"expert_stored{i}") for i in range(4)]
        waited = sem("waited")

        def rsqrt_guess(dve, v, y, t):
            yield dve.tensor_scalar(t.bitcast(I32), v.bitcast(I32), 1, None, ALU.logical_shift_right)
            yield dve.tensor_scalar(y.bitcast(I32), t.bitcast(I32), -1.0, float(0x5F3759DF), ALU.mult, ALU.add)

        def newton(dve, v, y, t):
            yield dve.tensor_tensor(t, y, y, ALU.mult)
            yield dve.scalar_tensor_tensor(out=t, in0=t, scalar=-0.5, in1=v, op0=ALU.mult, op1=ALU.mult)
            yield dve.scalar_tensor_tensor(out=y, in0=t, scalar=1.5, in1=y, op0=ALU.add, op1=ALU.mult)

        with ExitStack() as ph1:
            xn = sb(ph1, "xn", [P, ALL_TILES, D])
            nrm = sb(ph1, "nrm", [P, 2, TILES, D])
            w1_raw = sb(ph1, "w1_raw", [P, EXPERTS * FT, D])
            w2_raw = sb(ph1, "w2_raw", [P, EXPERTS, FF])
            w1T_hi = sb(ph1, "w1T_hi", [P, EXPERTS, FF], F32R)
            w1T_lo = sb(ph1, "w1T_lo", [P, EXPERTS, FF], F32R)
            w2T = sb(ph1, "w2T", [P, EXPERTS, FT, D])
            zeros = sb(ph1, "zeros", [P, SORTED * P // 13])
            wr_raw = sb(ph1, "wr_raw", [EXPERTS, D])
            b1_raw = sb(ph1, "b1_raw", [EXPERTS * FT, P])
            b2_all = sb(ph1, "b2_all", [P, EXPERTS, D])
            wrT = sb(ph1, "wrT", [P, EXPERTS])
            b1T = sb(ph1, "b1T", [P, EXPERTS * FT])
            br_all = sb(ph1, "br_all", [P, EXPERTS])
            agamma = sb(ph1, "agamma", [P, 1])
            ones = sb(ph1, "ones", [P, P])
            earlier = sb(ph1, "earlier", [P, P])
            before = sb(ph1, "before", [P, EXPERTS, EXPERTS])
            restart = sb(ph1, "restart", [P, EXPERTS, RT])
            tile_no = sb(ph1, "tile_no", [P, REGION])
            tile_no_int = sb(ph1, "tile_no_int", [P, REGION], I32)
            stats = sb(ph1, "stats", [P, TILES, 6])
            moments = sb(ph1, "moments", [P, TILES, 2])
            var2 = sb(ph1, "var2", [P, 2, TILES])
            root = sb(ph1, "root", [P, 2, TILES])
            tmp = sb(ph1, "tmp", [P, 2, TILES])
            nscale = sb(ph1, "nscale", [P, ALL_TILES])
            xnT = sb(ph1, "xnT", [P, 2, BANK])
            logit = sb(ph1, "logit", [P, RT, EXPERTS])
            more = sb(ph1, "more", [P, RT, EXPERTS, EXPERTS])
            same = sb(ph1, "same", [P, RT, EXPERTS, EXPERTS])
            rank = sb(ph1, "rank", [P, RT, EXPERTS])
            chosen = sb(ph1, "chosen", [P, RT, EXPERTS])
            pick = sb(ph1, "pick", [P, 2, RT, EXPERTS])
            prod = sb(ph1, "prod", [P, 2, RT, EXPERTS])
            two = sb(ph1, "two", [P, 2, RT])
            two_f = sb(ph1, "two_f", [P, 2, RT])
            gap = sb(ph1, "gap", [P, RT])
            upto = sb(ph1, "upto", [P, EXPERTS, RT])
            totals = sb(ph1, "totals", [P, EXPERTS, RT])
            tiles_int = sb(ph1, "tiles_int", [P, EXPERTS], I32)
            tiles_of = sb(ph1, "tiles_of", [P, EXPERTS])
            base = sb(ph1, "base", [P, EXPERTS])
            ends = sb(ph1, "ends", [P, EXPERTS])
            small = sb(ph1, "small", [P, EXPERTS, EXPERTS])
            slot = sb(ph1, "slot", [P, RT, EXPERTS])
            past = sb(ph1, "past", [P, REGION, EXPERTS])
            expert_f = sb(ph1, "expert_f", [P, REGION])
            tile_expert = sb(ph1, "tile_expert", [P, SORTED], I32)
            rows = sb(ph1, "rows", [P, 4, D])
            rowsT_hi = sb(ph1, "rowsT_hi", [P, 2, P], F32R)
            rowsT_lo = sb(ph1, "rowsT_lo", [P, 2, P], F32R)
            hidden = w1_raw[:, 0:2 * FT].rearrange("p (i f) d -> p i (f d)", i=2)
            hiddenT = w1_raw[:, 2 * FT:4 * FT].rearrange("p (i f) d -> p i f d", i=2)
            result = sb(ph1, "result", [P, 4, D])
            bank = [ps(ph1, f"bank{i}", [P, BANK]) for i in range(4)]
            obank = [ps(ph1, f"obank{i}", [P, D]) for i in range(2)]
            lbank = ps(ph1, "lbank", [P, RT, EXPERTS])
            tbank = ps(ph1, "tbank", [P, BANK])
            assert 2 * RT * EXPERTS <= BANK

            per_batch = TILES // GROUP
            units = [("wr", 0), ("b1", 0)]
            for b in range(2):
                for g in range(b * per_batch, (b + 1) * per_batch):
                    units += [("xn", g)]
            units += [("w1", e) for e in range(EXPERTS)] + [("w2", e) for e in range(EXPERTS)]
            for b in range(2):
                for g in range(b * per_batch, (b + 1) * per_batch):
                    units += [("n", g)]
            half_units = len(units)
            for b in range(2, BATCH):
                for g in range(b * per_batch, (b + 1) * per_batch):
                    units += [("xn", g)]
            for b in range(2, BATCH):
                for g in range(b * per_batch, (b + 1) * per_batch):
                    units += [("n", g)]
            reads, n = {}, 0
            for u, (kind, _) in enumerate(units):
                if kind in ("w1", "n"):
                    n += 1
                    reads[u] = n
            xn_units = [u for u, (kind, _) in enumerate(units) if kind == "xn"]

            def tbank_counts(n):
                return tbank[:, n * P:(n + 1) * P].rearrange("p (t e) -> p t e", e=EXPERTS)

            def freed(u):
                return u // 4 + 1

            UNROLL = 4
            FIRST, LOOPS = 3, (SORTED - 4) // UNROLL

            def expert_steps(eng, step):
                for j in range(FIRST):
                    step(j, j, None)
                with eng.Fori(0, LOOPS) as i:
                    for k in range(UNROLL):
                        step(i * UNROLL + (FIRST + k), FIRST + k, i)
                for j in range(FIRST + LOOPS * UNROLL, SORTED + 3):
                    step(j, j, None)

            def has(j, i, tile):
                return i is not None or 0 <= j + tile < SORTED

            def expert_of(eng, tile):
                return eng.value_load(tile_expert[0:1, bass.ds(tile, 1)], min_val=0, max_val=EXPERTS - 1)

            def times(k, i, tile):
                n = (k + tile) // 4
                return n if i is None else i + n

            with nc.Block() as block:

                @block.sync
                def _(sp):
                    for b in range(BATCH):
                        sp.dma_start(acc[:, b * TILES:(b + 1) * TILES],
                                     x_tiles[:, b * TILES:(b + 1) * TILES]).then_inc(x_loaded[b], 16)
                    sp.wait_ge(set_up, 1)
                    flat = sorted_x.rearrange("(p a) d -> p (a d)", p=P)
                    width = SORTED * P // 13
                    for i in range(13):
                        sp.dma_start(flat[:, i * width:(i + 1) * width], zeros[:]).then_inc(zeroed, 16)
                    src = sorted_x.rearrange("(j p) d -> p j d", p=P)

                    def load(j, k, i):
                        sp.wait_ge(rows_turned, j + 1)
                        sp.dma_start(rows[:, k % 4], src[:, bass.ds(j, 1)].rearrange("p j d -> p (j d)")
                                     ).then_inc(rows_loaded[k % 4], 16)

                    for r in range(REGIONS):
                        sp.wait_ge(scattered[r], 16 * 2 * RT)
                        j = r * REGION
                        while j % 4:
                            load(j, j, None)
                            j += 1
                        rounds = ((r + 1) * REGION - j) // 4
                        with sp.Fori(0, rounds) as i:
                            for k in range(4):
                                load(i * 4 + (j + k), k, i)
                        for j in range(j + rounds * 4, (r + 1) * REGION):
                            load(j, j, None)

                @block.gpsimd
                def _(pool):
                    pool.memset(zeros[:], 0.0).then_inc(set_up, 1)
                    pool.memset(ident[:], 1.0)
                    pool.memset(ones[:], 1.0)
                    pool.memset(earlier[:], 1.0)
                    pool.memset(restart[:], 1.0)
                    pool.iota(tile_no_int[:], [[1, REGION]], base=0, channel_multiplier=0)
                    pool.memset(before[:], 1.0).then_inc(set_up, 1)
                    pool.wait_ge(set_up, 2)
                    pool.memset(restart[:, :, 0:1], 0.0)
                    pool.affine_select(out=ident[:], in_=ident[:], pattern=[[1, P]], compare_op=ALU.is_equal,
                                       fill=0.0, base=0, channel_multiplier=-1).then_inc(set_up, 1)
                    pool.affine_select(out=earlier[:], in_=earlier[:], pattern=[[1, P]], compare_op=ALU.is_gt,
                                       fill=0.0, base=0, channel_multiplier=-1).then_inc(set_up, 1)
                    pool.affine_select(out=before[:], in_=before[:], pattern=[[1, EXPERTS], [-1, EXPERTS]],
                                       compare_op=ALU.is_gt, fill=0.0, base=0,
                                       channel_multiplier=0).then_inc(set_up, 1)
                    pool.tensor_copy(tile_no[:], tile_no_int[:]).then_inc(set_up, 1)

                    pool.wait_ge(zeroed, 16 * 13)
                    for r in range(REGIONS):
                        pool.wait_ge(slots_ready, r + 1)
                        for t in range(r * RT, (r + 1) * RT):
                            for n in range(2):
                                pool.indirect_dma_start(
                                    sorted_x, bass.IndirectOffsetOnAxis(ap=slots[:, n, t:t + 1], axis=0),
                                    xn[:, t], None).then_inc(scattered[r], 16)

                @block.scalar
                def _(act):
                    w1_src = w1.rearrange("e (f p) d -> p (e f) d", p=P)
                    with nc.allow_non_contiguous_dma(reason="one column of gamma"):
                        act.dma_start(agamma[:], attn_gamma.rearrange("(p a) -> p a", a=1)).then_inc(small_loaded, 16)
                    act.dma_start(wr_raw[:], w_router).then_inc(small_loaded, 16)
                    act.dma_start(b1_raw[:], b1.rearrange("e (f p) -> (e f) p", p=P)).then_inc(small_loaded, 16)
                    act.dma_start(br_all[:], b_router.partition_broadcast(P)).then_inc(small_loaded, 16)
                    half = EXPERTS * FT // 2
                    for i in range(2):
                        act.dma_start(w1_raw[:, i * half:(i + 1) * half],
                                      w1_src[:, i * half:(i + 1) * half]).then_inc(w1_loaded[i], 16)
                    act.dma_start(w2_raw[:], w2.rearrange("e d f -> d e f")).then_inc(w2_loaded, 16)
                    act.dma_start(b2_all[:], b2.partition_broadcast(P)).then_inc(small_loaded, 16)

                    def normed(b):
                        act.wait_ge(xn_ready, b + 1)
                        if b >= 2:
                            act.wait_ge(turned, units.index(("n", (b - 1) * per_batch - 1)) + 1)
                        for t in range(TILES):
                            ins = act.activation(nrm[:, b % 2, t], xn[:, b * TILES + t], ACT.Copy,
                                                 scale=nscale[:, b * TILES + t:b * TILES + t + 1])
                        ins.then_inc(nrm_ready, 1)

                    def evacuate(u):
                        kind, n = units[u]
                        src = bank[u % 4]
                        act.wait_ge(turned, u + 1)
                        cols = slice(n * BANK, (n + 1) * BANK)
                        if kind == "w1":
                            act.activation(w1T_hi[:, n], src[:], ACT.Copy).then_inc(act_read, 1)
                        elif kind == "n":
                            act.activation(nT[:, cols], src[:], ACT.Copy, scale=agamma[:, 0:1])
                            act.activation(nT_hi[:, cols], src[:], ACT.Copy,
                                           scale=agamma[:, 0:1]).then_inc(act_read, 1)
                        elif kind == "wr":
                            act.activation(wrT[:], src[:, 0:EXPERTS], ACT.Copy).then_inc(bank_free[u % 4], 1)
                        elif kind == "xn":
                            if n >= 2:
                                act.wait_ge(logits_done, n - 1)
                            act.activation(xnT[:, n % 2], src[:], ACT.Copy).then_inc(bank_free[u % 4], 1)
                        elif kind == "w2":
                            act.activation(w2T[:, n].rearrange("p f d -> p (f d)"), src[:],
                                           ACT.Copy).then_inc(bank_free[u % 4], 1)
                        elif kind == "b1":
                            act.activation(b1T[:], src[:, 0:EXPERTS * FT], ACT.Copy).then_inc(bank_free[u % 4], 1)

                    def exponentials(r):
                        act.wait_ge(exp_asked, r + 1)
                        act.activation(two[:, 1], gap[:], ACT.Exp).then_inc(exp_done, 1)

                    act.wait_ge(small_loaded, 16 * 5)
                    for u in range(half_units):
                        if u == units.index(("w1", 0)):
                            for b in range(2):
                                normed(b)
                        if u == units.index(("w2", 0)):
                            exponentials(0)
                        evacuate(u)
                    for u in range(half_units, len(units)):
                        if u == half_units + 4:
                            for b in range(2, BATCH):
                                normed(b)
                        evacuate(u)
                    exponentials(1)

                    def step(j, k, i):
                        if has(j, i, -1):
                            e = expert_of(act, j - 1)
                        if k == 0 and i is None:
                            rows_to_hi(0, 0)
                        if has(j, i, 1):
                            rows_to_hi(j + 1, k + 1)
                        if has(j, i, -1):
                            act.wait_ge(hidden_turned, j)
                            for f in range(FT):
                                ins = act.activation(hiddenT[:, (k - 1) % 2, f],
                                                     bank[2 + (k - 1) % 2][:, f * P:(f + 1) * P], ACT.Relu,
                                                     bias=b1T[:, bass.ds(e * FT + f, 1)])
                            ins.then_inc(relu_done, 1)
                        if has(j, i, -3):
                            act.wait_ge(expert_copied, j - 2 + 4)
                            act.dma_start(sorted_y[bass.ds((j - 3) * P, P), :],
                                          result[:, (k - 3) % 4]).then_inc(expert_stored[(k - 3) % 4], 16)

                    def rows_to_hi(j, k):
                        act.wait_ge(rows_turned, j + 1 + 4)
                        act.activation(rowsT_hi[:, k % 2], tbank[:, 0:P], ACT.Copy).then_inc(rows_hi, 1)

                    act.wait_ge(set_up, 7)
                    act.sem_inc(waited, 1)
                    expert_steps(act, step)
                    for n in range(4):
                        act.wait_ge(expert_stored[n], 16 * (1 + len(range(n, SORTED, 4))))

                @block.vector
                def _(dve):
                    steps = [0]

                    def then(ins):
                        steps[0] += 1
                        ins.then_inc(dve_step, 1)
                        dve.wait_ge(dve_step, steps[0])

                    dve.sem_inc(rows_turned, 4)
                    dve.sem_inc(expert_copied, 4)
                    for n in range(4):
                        dve.sem_inc(expert_stored[n], 16)

                    def layernorm(b):
                        tiles = slice(b * TILES, (b + 1) * TILES)
                        dve.wait_ge(x_loaded[b], 16)
                        for t in range(TILES):
                            ins = dve.bn_stats(stats[:, t], acc[:, b * TILES + t])
                        then(ins)
                        for t in range(TILES):
                            ins = dve.bn_aggr(moments[:, t], stats[:, t])
                        then(ins)
                        dve.tensor_scalar(mean[:, tiles], moments[:, :, 0], 1.0, None, ALU.mult)
                        dve.tensor_scalar(var2[:, 0], moments[:, :, 1], LN_EPS, None, ALU.add)
                        then(dve.tensor_scalar(var2[:, 1], moments[:, :, 1], float(D), TINY, ALU.mult, ALU.max))
                        for ins in rsqrt_guess(dve, var2[:], root[:], tmp[:]):
                            then(ins)
                        for _ in range(3):
                            for ins in newton(dve, var2[:], root[:], tmp[:]):
                                then(ins)
                        dve.tensor_scalar(rstd[:, tiles], root[:, 0], 1.0, None, ALU.mult)
                        then(dve.tensor_tensor(tmp[:, 0], root[:, 1], var2[:, 1], ALU.mult))
                        then(dve.tensor_tensor(tmp[:, 0], tmp[:, 0], root[:, 0], ALU.mult))
                        then(dve.tensor_scalar(tmp[:, 0], tmp[:, 0], RMS_EPS, None, ALU.max))
                        then(dve.reciprocal(tmp[:, 1], tmp[:, 0]))
                        then(dve.tensor_scalar(nscale[:, tiles], tmp[:, 1], float(D) ** 0.5, None, ALU.mult))
                        for t in range(b * TILES, (b + 1) * TILES):
                            ins = dve.tensor_scalar(xn[:, t], acc[:, t], mean[:, t:t + 1], rstd[:, t:t + 1],
                                                    ALU.subtract, ALU.mult)
                        ins.then_inc(xn_ready, 1)

                    def lower(u):
                        kind, n = units[u]
                        src = bank[u % 4]
                        if u not in reads:
                            return
                        dve.wait_ge(act_read, reads[u])
                        if kind == "w1":
                            dve.tensor_tensor(w1T_lo[:, n], src[:], w1T_hi[:, n].bitcast(F32),
                                              ALU.subtract).then_inc(bank_free[u % 4], 1)
                        else:
                            cols = slice(n * BANK, (n + 1) * BANK)
                            dve.scalar_tensor_tensor(out=nT_lo[:, cols], in0=src[:], scalar=agamma[:, 0:1],
                                                     in1=nT_hi[:, cols].bitcast(F32), op0=ALU.mult,
                                                     op1=ALU.subtract).then_inc(bank_free[u % 4], 1)

                    def router(r):
                        over = [P, RT, EXPERTS]
                        shape4 = [P, RT, EXPERTS, EXPERTS]
                        dve.wait_ge(logits_done, (r + 1) * RT // GROUP)
                        then(dve.tensor_tensor(logit[:], lbank[:], br_all[:].unsqueeze(1).broadcast_to(over),
                                               ALU.add))
                        mine = logit[:].unsqueeze(3).broadcast_to(shape4)
                        other = logit[:].unsqueeze(2).broadcast_to(shape4)
                        dve.tensor_tensor(more[:], other, mine, ALU.is_gt)
                        then(dve.tensor_tensor(same[:], other, mine, ALU.is_equal))
                        then(dve.tensor_tensor(same[:], same[:], before[:].unsqueeze(1).broadcast_to(shape4),
                                               ALU.mult))
                        then(dve.tensor_tensor(more[:], more[:], same[:], ALU.add))
                        then(dve.tensor_reduce(rank[:], more[:], AX_X, ALU.add))
                        dve.tensor_scalar(chosen[:], rank[:], 1.5, None, ALU.is_lt).then_inc(chosen_ready, 1)
                        dve.tensor_scalar(pick[:, 0], rank[:], 0.0, None, ALU.is_equal)
                        then(dve.tensor_scalar(pick[:, 1], rank[:], 1.0, None, ALU.is_equal))
                        then(dve.tensor_tensor(prod[:], pick[:], logit[:].unsqueeze(1).broadcast_to(
                            [P, 2, RT, EXPERTS]), ALU.mult))
                        then(dve.tensor_reduce(two[:], prod[:], AX_X, ALU.add))
                        dve.tensor_tensor(gap[:], two[:, 1], two[:, 0], ALU.subtract).then_inc(exp_asked, 1)

                    def places(r):
                        toks = slice(r * RT, (r + 1) * RT)
                        dve.wait_ge(counted, r + 1)
                        dve.tensor_copy(totals[:], tbank_counts(1).rearrange("p t e -> p e t"))
                        then(dve.tensor_copy(slot[:], tbank_counts(0)))
                        then(dve.tensor_tensor_scan(upto[:].rearrange("p e t -> p (e t)"),
                                                    restart[:].rearrange("p e t -> p (e t)"),
                                                    totals[:].rearrange("p e t -> p (e t)"),
                                                    0.0, ALU.mult, ALU.add))
                        then(dve.tensor_scalar(tiles_int[:], upto[:, :, RT - 1], 1.0 / P,
                                               (P - 1) / P - 0.5 + 0.5 / P, ALU.mult, ALU.add))
                        then(dve.tensor_copy(tiles_of[:], tiles_int[:]))
                        then(dve.tensor_tensor(small[:], before[:], tiles_of[:].unsqueeze(1).broadcast_to(
                            [P, EXPERTS, EXPERTS]), ALU.mult))
                        then(dve.tensor_reduce(base[:], small[:], AX_X, ALU.add))
                        then(dve.tensor_tensor(ends[:], base[:], tiles_of[:], ALU.add))
                        then(dve.tensor_scalar(base[:], base[:], float(P), float(r * REGION * P), ALU.mult, ALU.add))
                        then(dve.tensor_tensor(upto[:], upto[:], totals[:], ALU.subtract))
                        then(dve.tensor_tensor(upto[:], upto[:], base[:].unsqueeze(2).broadcast_to(
                            [P, EXPERTS, RT]), ALU.add))
                        then(dve.tensor_tensor(slot[:], slot[:], upto[:].rearrange("p e t -> p t e"), ALU.add))
                        then(dve.tensor_tensor(prod[:], pick[:], slot[:].unsqueeze(1).broadcast_to(
                            [P, 2, RT, EXPERTS]), ALU.mult))
                        then(dve.tensor_reduce(two_f[:], prod[:], AX_X, ALU.add))
                        dve.tensor_copy(slots[:, :, toks], two_f[:]).then_inc(slots_ready, 1)
                        over = [P, REGION, EXPERTS]
                        dve.wait_ge(set_up, 6)
                        then(dve.tensor_tensor(past[:], tile_no[:].unsqueeze(2).broadcast_to(over),
                                               ends[:].unsqueeze(1).broadcast_to(over), ALU.is_ge))
                        then(dve.tensor_reduce(expert_f[:], past[:], AX_X, ALU.add))
                        then(dve.tensor_scalar(tile_expert[:, r * REGION:(r + 1) * REGION], expert_f[:],
                                               float(EXPERTS - 1), None, ALU.min))
                        dve.wait_ge(exp_done, r + 1)
                        then(dve.tensor_scalar(gap[:], two[:, 1], 1.0, None, ALU.add))
                        then(dve.reciprocal(weights[:, 0, toks], gap[:]))
                        then(dve.tensor_tensor(weights[:, 1, toks], two[:, 1], weights[:, 0, toks], ALU.mult))

                    dve.wait_ge(small_loaded, 16 * 5)
                    layernorm(0)
                    layernorm(1)
                    dve.wait_ge(set_up, 5)
                    router(0)
                    for u in range(units.index(("w1", 4))):
                        lower(u)
                    places(0)
                    layernorm(2)
                    for u in range(units.index(("w1", 4)), half_units):
                        lower(u)
                        if u == units.index(("w1", 5)):
                            layernorm(3)
                    for u in range(half_units, half_units + 4):
                        lower(u)
                    router(1)
                    places(1)
                    dve.sem_inc(set_up, 1)
                    for u in range(half_units + 4, len(units)):
                        lower(u)

                    def rows_to_lo(j, k):
                        dve.wait_ge(rows_hi, j + 1)
                        dve.tensor_tensor(rowsT_lo[:, k % 2], tbank[:, 0:P], rowsT_hi[:, k % 2].bitcast(F32),
                                          ALU.subtract).then_inc(rows_split, 1)

                    def step(j, k, i):
                        if has(j, i, -2):
                            e = expert_of(dve, j - 2)
                        if k == 0 and i is None:
                            rows_to_lo(0, 0)
                        if has(j, i, 1):
                            rows_to_lo(j + 1, k + 1)
                        if has(j, i, 0):
                            dve.wait_ge(hidden_done, j + 1)
                            dve.tensor_copy(hidden[:, k % 2], bank[k % 2][:]).then_inc(hidden_copied, 1)
                        if has(j, i, -2):
                            dve.wait_ge(expert_stored[(k - 2) % 4], (times(k, i, -2) + 1) * 16)
                            dve.wait_ge(expert_out, j - 1)
                            dve.tensor_tensor(result[:, (k - 2) % 4], obank[k % 2][:],
                                              b2_all[:, bass.ds(e, 1)].rearrange("p e d -> p (e d)"),
                                              ALU.add).then_inc(expert_copied, 1)

                    expert_steps(dve, step)

                @block.tensor
                def _(pe):
                    def turn(u):
                        kind, n = units[u]
                        if u >= 4:
                            pe.wait_ge(bank_free[u % 4], freed(u - 4))
                        dst = bank[u % 4]
                        if kind == "w1":
                            if n % (EXPERTS // 2) == 0:
                                pe.wait_ge(w1_loaded[n // (EXPERTS // 2)], 16)
                            for f in range(FT):
                                ins = pe.transpose(dst[:, f * P:(f + 1) * P], w1_raw[:, n * FT + f], ident[:])
                        elif kind == "w2":
                            if n == 0:
                                pe.wait_ge(w2_loaded, 16)
                            for f in range(FT):
                                ins = pe.transpose(dst[:, f * P:(f + 1) * P], w2_raw[:, n, f * P:(f + 1) * P],
                                                   ident[:])
                        elif kind == "wr":
                            ins = pe.transpose(dst[:, 0:EXPERTS], wr_raw[:], ident[0:EXPERTS, 0:EXPERTS])
                        elif kind == "b1":
                            ins = pe.transpose(dst[:, 0:EXPERTS * FT], b1_raw[:],
                                               ident[0:EXPERTS * FT, 0:EXPERTS * FT])
                        else:
                            b = n // per_batch
                            pe.wait_ge(xn_ready if kind == "xn" else nrm_ready, b + 1)
                            for q in range(GROUP):
                                t = n * GROUP + q
                                src = xn[:, t] if kind == "xn" else nrm[:, b % 2, t % TILES]
                                ins = pe.transpose(dst[:, q * P:(q + 1) * P], src, ident[:])
                        ins.then_inc(turned, 1)

                    def logits(g):
                        u = units.index(("xn", g))
                        pe.wait_ge(bank_free[u % 4], freed(u))
                        if g == RT // GROUP:
                            pe.wait_ge(chosen_ready, 1)
                        for q in range(GROUP):
                            ins = pe.matmul(lbank[:, (g * GROUP + q) % RT], xnT[:, g % 2, q * P:(q + 1) * P], wrT[:],
                                            start=True, stop=True)
                        ins.then_inc(logits_done, 1)

                    def count(r):
                        pe.wait_ge(chosen_ready, r + 1)
                        pe.matmul(tbank_counts(0), earlier[:], chosen[:], start=True, stop=True)
                        pe.matmul(tbank_counts(1), ones[:], chosen[:], start=True, stop=True).then_inc(counted, 1)

                    pe.wait_ge(small_loaded, 16 * 5)
                    pe.wait_ge(set_up, 5)
                    groups = RT // GROUP
                    for u in range(2 + groups):
                        turn(u)
                        if u >= 3:
                            logits(u - 3)
                    logits(groups - 1)
                    for u in range(2 + groups, half_units):
                        if u == units.index(("w1", 4)):
                            count(0)
                        turn(u)
                    for g in range(groups):
                        turn(half_units + g)
                        if g:
                            logits(groups + g - 1)
                    logits(2 * groups - 1)
                    for u in range(half_units + groups, len(units)):
                        if u == half_units + groups + 2:
                            pe.wait_ge(slots_ready, 1)
                            count(1)
                        turn(u)
                    for u in range(len(units) - 4, len(units)):
                        pe.wait_ge(bank_free[u % 4], freed(u))
                    pe.wait_ge(set_up, 7)
                    pe.sem_inc(waited, 1)

                    def turn_rows(j, k, i):
                        pe.wait_ge(rows_loaded[k % 4], (times(k, i, 0) + 1) * 16)
                        pe.transpose(tbank[:, 0:P], rows[:, k % 4], ident[:]).then_inc(rows_turned, 1)

                    def step(j, k, i):
                        if has(j, i, 0):
                            e_in = expert_of(pe, j)
                        if has(j, i, -2):
                            e_out = expert_of(pe, j - 2)
                        if k == 0 and i is None:
                            turn_rows(0, 0, None)
                        if has(j, i, 1):
                            pe.wait_ge(rows_split, j + 1)
                            turn_rows(j + 1, k + 1, i)
                        if has(j, i, -1):
                            pe.wait_ge(hidden_copied, j)
                            for f in range(FT):
                                ins = pe.transpose(bank[2 + (k - 1) % 2][:, f * P:(f + 1) * P],
                                                   hidden[:, (k - 1) % 2, f * P:(f + 1) * P], ident[:])
                            ins.then_inc(hidden_turned, 1)
                        if has(j, i, 0):
                            pe.wait_ge(rows_split, j + 1)
                            w_hi = w1T_hi[:, bass.ds(e_in, 1)].rearrange("p e f -> p (e f)")
                            w_lo = w1T_lo[:, bass.ds(e_in, 1)].rearrange("p e f -> p (e f)")
                            pe.matmul(bank[k % 2][:], rowsT_hi[:, k % 2], w_hi, start=True, stop=False)
                            pe.matmul(bank[k % 2][:], rowsT_hi[:, k % 2], w_lo, start=False, stop=False)
                            pe.matmul(bank[k % 2][:], rowsT_lo[:, k % 2], w_hi, start=False,
                                      stop=True).then_inc(hidden_done, 1)
                        if has(j, i, -2):
                            pe.wait_ge(relu_done, j - 1)
                            pe.wait_ge(expert_copied, j - 3 + 4)
                            for f in range(FT):
                                ins = pe.matmul(obank[k % 2][:], hiddenT[:, (k - 2) % 2, f],
                                                w2T[:, bass.ds(e_out, 1), f].rearrange("p e d -> p (e d)"),
                                                start=(f == 0), stop=(f == FT - 1))
                            ins.then_inc(expert_out, 1)

                    expert_steps(pe, step)

        qkv_loaded = sem("qkv_loaded")
        wout_loaded = sem("wout_loaded")
        wqk_hi_done = sem("wqk_hi_done")
        wqk_split = sem("wqk_split")
        mask_zeroed = sem("mask_zeroed")
        attn_consts = sem("attn_consts")
        max_scores = sem("max_scores")
        max_taken = sem("max_taken")
        max_split = sem("max_split")
        max_step = sem("max_step")
        misc_ready = sem("misc_ready")
        hi_done = sem("hi_done")
        lo_done = sem("lo_done")
        v_hi_done = sem("v_hi_done")
        v_done = sem("v_done")
        full_split = sem("full_split")
        diag_split = sem("diag_split")
        copies_done = sem("copies_done")
        shift_done = sem("shift_done")
        scores_ready = sem("scores_ready")
        probs_ready = sem("probs_ready")
        diag_masked = sem("diag_masked")
        pv_done = sem("pv_done")
        heads_out = [sem(f"heads_out{i}") for i in range(2)]
        recip_done = sem("recip_done")
        y_added = sem("y_added")
        stored = sem("stored")
        small2_loaded = sem("small2_loaded")
        group_taken = sem("group_taken")
        gathered = sem("gathered")
        x_again = sem("x_again")
        comb_step = sem("comb_step")

        with ExitStack() as ph2:
            q_a = [[sb(ph2, f"q_a{i}{s}", [P, SEQ], F32R) for s in range(2)] for i in range(2)]
            k_a = [[sb(ph2, f"k_a{i}{s}", [P, SEQ], F32R) for s in range(2)] for i in range(2)]
            q_b = [[sb(ph2, f"q_b{i}{s}", [HEAD + 2, SEQ], F32R) for s in range(2)] for i in range(2)]
            k_b = [[sb(ph2, f"k_b{i}{s}", [HEAD + 2, SEQ], F32R) for s in range(2)] for i in range(2)]
            v_hi = [sb(ph2, f"v_hi{i}", [P, TILES, 2, HEAD + 1], F32R) for i in range(2)]
            v_lo = [sb(ph2, f"v_lo{i}", [P, TILES, 2, HEAD], F32R) for i in range(2)]
            RING = 4
            probs = sb(ph2, "probs", [P, RING, BANK])
            p_hi = sb(ph2, "p_hi", [P, RING, BANK], F32R)
            p_lo = sb(ph2, "p_lo", [P, RING, BANK], F32R)
            heads = sb(ph2, "heads", [HEAD + 1, 2, SEQ])
            w_raw = sb(ph2, "w_raw", [P, 3, P])
            wqk_hi = sb(ph2, "wqk_hi", [P, 2, P], F32R)
            wqk_lo = sb(ph2, "wqk_lo", [P, 2, P], F32R)
            wo = sb(ph2, "wo", [HEAD + 1, 2, D + 1])
            mask = sb(ph2, "mask", [P, SEQ])
            unread = sb(ph2, "unread", [P, 2, SEQ], BF16)
            row_max = sb(ph2, "row_max", [P, 2, TILES])
            shift = sb(ph2, "shift", [P, 2, TILES, 2], F32R)
            rden = sb(ph2, "rden", [P, 2, 4])
            fgamma = sb(ph2, "fgamma", [P, D])
            fbeta = sb(ph2, "fbeta", [P, D])
            places = sb(ph2, "places", [P, 2 * GROUP], U32)
            two_y = sb(ph2, "two_y", [P, 2 * GROUP, D])
            x_row = sb(ph2, "x_row", [P, GROUP, D])
            gstat = sb(ph2, "gstat", [P, GROUP, 6])
            gmom = sb(ph2, "gmom", [P, GROUP, 2])
            gvar = sb(ph2, "gvar", [P, 3, GROUP])
            gsc = sb(ph2, "gsc", [P, 4, GROUP])
            max_ps = ps(ph2, "max_ps", [P, SEQ])
            score_ps = [ps(ph2, f"score_ps{i}", [P, BANK]) for i in range(2)]
            head_ps = ps(ph2, "head_ps", [P, SEQ])
            misc_ps = [ps(ph2, f"misc_ps{i}", [P, BANK]) for i in range(2)]

            chunks = [(half, j, max(half * BANK, j * P))
                      for half, keys in ((0, (0, 3, 1, 2)), (1, (0, 7, 1, 6, 2, 5, 4, 3))) for j in keys]
            LAST = [3, 11]
            CH = len(chunks)
            DIAG = [q0 == j * P for _, j, q0 in chunks]
            LAG = 3
            G = BATCH * 2
            MAX_AT = [1, 2, 3, 4, 5, 7, 9, 11]
            PROJECT_AT = [{0: 0, 1: 1, 3: 2, 5: 3}, {1: 4, 5: 5}]
            GATHER_AT = [(1, c) for c in (6, 7, 8, 9, 10, 11)] + [(2, c) for c in (1, 3, 5)]
            COMBINE_AT = [(3, c) for c in (0, 3, 6, 8)] + [(4, c) for c in (0, 3, 6, 8)] + [(5, c) for c in (0, 3, 6)]
            COMBINE_STEPS = 22
            Y_AT = [4, 7, 9]
            y_units = [(0, 3), (3, 3), (6, 2)]

            def plan(last):
                order = []
                for g in range(G):
                    more = not (last and g == G - 1)
                    for c in range(CH):
                        order.append(("score", g, c))
                        if c >= LAG - 1:
                            order.append(("low", g, c - LAG + 1))
                        elif g:
                            order.append(("low", g - 1, CH + c - LAG + 1))
                        if more and c in MAX_AT:
                            order.append(("max", g + 1, MAX_AT.index(c)))
                        if c in PROJECT_AT[g % 2] and not (last and g >= G - 2):
                            order.append(("project", g // 2 + 1, PROJECT_AT[g % 2][c]))
                        if g and c in Y_AT:
                            order.append(("y", g - 1, Y_AT.index(c)))
                        if more and c == 8:
                            order.append(("shift", g + 1, 0))
                        if c == 2:
                            order.append(("shift", g, 1))
                        if (g, c) in GATHER_AT:
                            order.append(("gather", GATHER_AT.index((g, c)), 0))
                        if (g, c) in COMBINE_AT:
                            order.append(("combine", COMBINE_AT.index((g, c)), 0))
                        if g == G - 3 and c == 10 and not last:
                            order.append(("weights", 0, 0))
                        if c >= LAG:
                            order.append(("pv", g, c - LAG))
                        elif g:
                            order.append(("pv", g - 1, CH + c - LAG))
                for c in range(CH - LAG, CH):
                    if c > CH - LAG:
                        order.append(("low", G - 1, c))
                    order.append(("pv", G - 1, c))
                for n in range(len(y_units)):
                    order.append(("y", G - 1, n))
                return numbered(order)

            def numbered(order):
                n, out_ = 0, []
                for o in order:
                    misc = o[0] in ("project", "shift", "y")
                    out_.append((*o, n if misc else None))
                    n += misc
                return out_

            first = numbered([("project", 0, n) for n in range(6)]
                             + [("max", 0, t) for t in range(TILES)] + [("shift", 0, 0)])
            MISC0 = sum(o[-1] is not None for o in first)
            MISC = sum(o[-1] is not None for o in plan(False))
            assert MISC % 2 == 0
            first_units = [o[:3] for o in first if o[-1] is not None]

            def n_max(hp, g, t):
                return hp * (G * TILES) + (g * TILES + t)

            def n_chunk(hp, g, c):
                return hp * (G * CH) + (g * CH + c)

            def n_diag(hp, g, c):
                return hp * (G * sum(DIAG)) + (g * sum(DIAG) + sum(DIAG[:c]))

            def n_full(hp, g, c):
                return hp * (G * (CH - sum(DIAG))) + (g * (CH - sum(DIAG)) + c - sum(DIAG[:c]))

            def n_misc(hp, u, start):
                return (0 if start else MISC0) + hp * MISC + u

            def bank_of(u, start):
                return (u + MISC0) % 2 if start else u % 2

            def n_half(hp, g, half):
                return hp * (G * 2) + (g * 2 + half)

            def n_y(hp, g, n):
                return hp * (G * len(y_units)) + (g * len(y_units) + n)

            def n_batch(hp, p):
                return hp * BATCH + p

            def run(eng, walk):
                with eng.Fori(0, PAIRS - 1) as hp:
                    walk(hp, plan(False), False)
                walk(PAIRS - 1, plan(True), True)

            with nc.Block() as block:

                @block.sync
                def _(sp):
                    def weights(hp):
                        src = w_qkv.rearrange("d (s h c) -> d s h c", s=3, c=P)
                        sp.dma_start(w_raw[:], src[:, :, bass.ds(hp, 1)].rearrange("d s h c -> d (s h) c")
                                     ).then_inc(qkv_loaded, 16)

                    def out_weights(hp):
                        src = w_out.rearrange("(h s c) d -> c h s d", s=2, c=HEAD)
                        sp.dma_start(wo[0:HEAD, :, 0:D], src[:, bass.ds(hp, 1)].rearrange("c h s d -> c (h s) d")
                                     ).then_inc(wout_loaded, 16)

                    def copies(hp, p):
                        i = p % 2
                        sp.wait_ge(hi_done, n_batch(hp, p) * 8 + 8)
                        for s in range(2):
                            k_hi, q_hi = k_a[i][s][0:HEAD, :].bitcast(F32), q_a[i][s][0:HEAD, :].bitcast(F32)
                            sp.dma_start(k_a[i][s][HEAD:P, :].bitcast(F32), k_hi).then_inc(copies_done, 16)
                            sp.dma_start(q_b[i][s][0:HEAD, :].bitcast(F32), q_hi).then_inc(copies_done, 16)

                    weights(0)
                    sp.dma_start(fgamma[:], ffn_gamma.partition_broadcast(P)).then_inc(small2_loaded, 16)
                    sp.dma_start(fbeta[:], ffn_beta.partition_broadcast(P)).then_inc(small2_loaded, 16)
                    sp.wait_ge(attn_consts, 2)
                    out_weights(0)
                    copies(0, 0)

                    def walk(hp, order, last):
                        for o in order:
                            if o[0] == "project" and o[2] == 3:
                                copies(hp, o[1])
                            if o[0] == "gather" and o[1] == 0:
                                sp.wait_ge(group_taken, hp + 1)
                                sp.dma_start(x_row[:], x_tiles[:, bass.ds(hp * GROUP, GROUP)]).then_inc(x_again, 16)
                            if o[0] == "project" and o[1] == BATCH - 1 and o[2] == 5 and not last:
                                sp.wait_ge(misc_ready, n_misc(hp, o[3], False) + 1)
                                weights(hp + 1)
                        if not last:
                            sp.wait_ge(misc_ready, n_misc(hp, order[-1][3], False) + 1)
                            out_weights(hp + 1)
                        else:
                            sp.wait_ge(comb_step, PAIRS * COMBINE_STEPS)
                            for p in range(BATCH):
                                sp.wait_ge(y_added, n_y(hp, 2 * p + 1, len(y_units) - 1) + 2)
                                sp.dma_start(out_tiles[:, p * TILES:(p + 1) * TILES],
                                             acc[:, p * TILES:(p + 1) * TILES]).then_inc(stored, 16)
                            sp.wait_ge(stored, 16 * BATCH)

                    run(sp, walk)

                @block.gpsimd
                def _(pool):
                    pool.memset(wo[:], 0.0).then_inc(mask_zeroed, 1)
                    pool.memset(mask[:], 0.0).then_inc(mask_zeroed, 1)
                    for i in range(2):
                        pool.memset(v_hi[i][:, :, :, HEAD:HEAD + 1].bitcast(F32), 1.0).then_inc(mask_zeroed, 1)
                    pool.wait_ge(mask_zeroed, 4)
                    tri = mask[:, SEQ - P:SEQ]
                    pool.affine_select(out=tri, in_=tri, pattern=[[-1, P]], compare_op=ALU.is_ge, fill=MASKED,
                                       base=0, channel_multiplier=1).then_inc(attn_consts, 1)
                    pool.wait_ge(attn_consts, 1)
                    pool.memset(wo[HEAD:HEAD + 1, :, D:D + 1], 1.0).then_inc(attn_consts, 1)
                    n = 2
                    for i in range(2):
                        for s in range(2):
                            pool.wait_ge(attn_consts, n)
                            pool.memset(k_b[i][s][HEAD:HEAD + 2, :].bitcast(F32), 1.0).then_inc(attn_consts, 1)
                            n += 1
                    pool.wait_ge(attn_consts, n)

                    def walk(hp, order, last):
                        for o in order:
                            if o[0] == "gather" and o[1]:
                                n = o[1] - 1
                                pool.wait_ge(group_taken, hp + 1)
                                pool.sem_inc(waited, 1)
                                pool.indirect_dma_start(
                                    two_y[:, n], None, sorted_y,
                                    bass.IndirectOffsetOnAxis(ap=places[:, n:n + 1], axis=0)).then_inc(gathered, 16)
                            if o[0] != "score":
                                continue
                            _, g, c, _ = o
                            slot = (g * CH + c) % RING
                            pool.wait_ge(probs_ready, n_chunk(hp, g, c) + 1 + 2)
                            if DIAG[c]:
                                pool.sem_inc(waited, 1)
                                for tile in (probs[:, slot, 0:P], p_hi[:, slot, 0:P].bitcast(F32)):
                                    out_tile = p_hi[:, slot, 0:P] if tile.tensor.name == "p_hi" else tile
                                    ins = pool.affine_select(out=out_tile, in_=tile, pattern=[[1, P]],
                                                             compare_op=ALU.is_ge, fill=0.0, base=0,
                                                             channel_multiplier=-1)
                                ins.then_inc(diag_masked, 1)
                            else:
                                pool.tensor_tensor(p_lo[:, slot], probs[:, slot], p_hi[:, slot].bitcast(F32),
                                                   ALU.subtract).then_inc(full_split, 1)

                    run(pool, walk)

                @block.scalar
                def _(act):
                    act.sem_inc(probs_ready, 2)
                    act.sem_inc(heads_out[0], 1)
                    act.sem_inc(heads_out[1], 1)

                    def w_hi(hp):
                        act.wait_ge(qkv_loaded, hp * 16 + 16)
                        act.activation(wqk_hi[:], w_raw[:, 0:2], ACT.Copy).then_inc(wqk_hi_done, 1)

                    def project(hp, p, n, u, start):
                        i = p % 2
                        act.wait_ge(misc_ready, n_misc(hp, u, start) + 1)
                        src = misc_ps[bank_of(u, start)]
                        if n < 4:
                            dst, cols = (q_a, k_a)[n // 2][i], slice(n % 2 * BANK, (n % 2 + 1) * BANK)
                            for s in range(2):
                                act.activation(dst[s][0:HEAD, cols], src[s * HEAD:(s + 1) * HEAD, :],
                                               ACT.Copy).then_inc(hi_done, 1)
                        else:
                            t = (n - 4) * GROUP
                            act.activation(v_hi[i][:, t:t + GROUP, :, 0:HEAD],
                                           src[:].rearrange("p (t s c) -> p t s c", s=2, c=HEAD),
                                           ACT.Copy).then_inc(v_hi_done, 1)

                    def shifts(hp, g, half, u, start):
                        act.wait_ge(misc_ready, n_misc(hp, u, start) + 1)
                        dst = q_b[g // 2 % 2][g % 2]
                        act.activation(dst[HEAD:HEAD + 2, half * BANK:(half + 1) * BANK], misc_ps[bank_of(u, start)][0:2, :],
                                       ACT.Copy).then_inc(shift_done, 1)

                    w_hi(0)
                    for o in first:
                        if o[0] == "project":
                            project(0, o[1], o[2], o[3], True)
                        elif o[0] == "shift":
                            shifts(0, o[1], o[2], o[3], True)

                    def walk(hp, order, last):
                        for o in order:
                            kind, g, c, u = o
                            if kind == "score":
                                half, j, q0 = chunks[c]
                                width = (half + 1) * BANK - q0
                                act.wait_ge(scores_ready, n_chunk(hp, g, c) + 1)
                                act.wait_ge(pv_done, n_chunk(hp, g, c) + 1)
                                for p in (probs, p_hi):
                                    ins = act.activation(p[:, (g * CH + c) % RING, 0:width],
                                                         score_ps[(g * CH + c) % 2][:, 0:width], ACT.Exp,
                                                         scale=SCALE)
                                ins.then_inc(probs_ready, 1)
                            elif kind == "project":
                                project(hp, g, c, u, False)
                            elif kind == "weights":
                                w_hi(hp + 1)
                            elif kind == "shift":
                                shifts(hp, g, c, u, False)
                            elif kind == "pv" and c in LAST:
                                half = LAST.index(c)
                                cols = slice(half * BANK, (half + 1) * BANK)
                                act.wait_ge(pv_done, n_chunk(hp, g, c) + 1 + RING)
                                act.activation(heads[:, g % 2, cols], head_ps[0:HEAD + 1, cols],
                                               ACT.Copy).then_inc(heads_out[half], 1)

                    run(act, walk)

                @block.vector
                def _(dve):
                    def w_lo(hp):
                        dve.wait_ge(wqk_hi_done, hp + 1)
                        dve.tensor_tensor(wqk_lo[:], w_raw[:, 0:2], wqk_hi[:].bitcast(F32),
                                          ALU.subtract).then_inc(wqk_split, 1)

                    def project(hp, p, n, u, start):
                        i = p % 2
                        if n >= 4:
                            t = (n - 4) * GROUP
                            dve.wait_ge(v_hi_done, n_batch(hp, p) * 2 + (n - 3))
                            dve.tensor_tensor(v_lo[i][:, t:t + GROUP],
                                              misc_ps[bank_of(u, start)][:].rearrange("p (t s c) -> p t s c", s=2, c=HEAD),
                                              v_hi[i][:, t:t + GROUP, :, 0:HEAD].bitcast(F32),
                                              ALU.subtract).then_inc(v_done, 1)
                            return
                        cols = slice(n % 2 * BANK, (n % 2 + 1) * BANK)
                        src = misc_ps[bank_of(u, start)]
                        for s in range(2):
                            dve.wait_ge(hi_done, n_batch(hp, p) * 8 + (n * 2 + s + 1))
                            hi = (q_a, k_a)[n // 2][i][s][0:HEAD, cols].bitcast(F32)
                            lo = q_a[i][s][HEAD:P, cols] if n < 2 else k_b[i][s][0:HEAD, cols]
                            ins = dve.tensor_tensor(lo, src[s * HEAD:(s + 1) * HEAD, :], hi, ALU.subtract)
                        ins.then_inc(lo_done, 1)

                    def maximum(hp, g, t):
                        width = (t + 1) * P
                        src = max_ps[:, t % 2 * BANK:t % 2 * BANK + width] if t < 4 else max_ps[:, 0:width]
                        dve.wait_ge(max_scores, n_max(hp, g, t) + 1)
                        if g or t >= 2:
                            dve.wait_ge(max_taken, n_max(hp, g, t) - 1)
                        dve.sem_inc(waited, 1)
                        dve.tensor_tensor_reduce(out=unread[:, t % 2, 0:width], in0=src, in1=mask[:, SEQ - width:SEQ],
                                                 scale=1.0, scalar=MASKED, op0=ALU.add, op1=ALU.max,
                                                 accum_out=row_max[:, g % 2, t:t + 1]).then_inc(max_taken, 1)
                        if t % 4 == 3:
                            rows = slice(t - 3, t + 1)
                            dve.wait_ge(max_taken, n_max(hp, g, t) + 1)
                            dve.tensor_scalar(shift[:, g % 2, rows, 0], row_max[:, g % 2, rows], -1.0, None,
                                              ALU.mult).then_inc(max_step, 1)
                            dve.wait_ge(max_step, n_half(hp, g, t // 4) + 1)
                            dve.scalar_tensor_tensor(out=shift[:, g % 2, rows, 1], in0=row_max[:, g % 2, rows],
                                                     scalar=-1.0, in1=shift[:, g % 2, rows, 0].bitcast(F32),
                                                     op0=ALU.mult, op1=ALU.subtract).then_inc(max_split, 1)

                    steps = [0]

                    def then(hp, ins):
                        steps[0] += 1
                        ins.then_inc(comb_step, 1)
                        dve.wait_ge(comb_step, hp * COMBINE_STEPS + steps[0])
                        dve.sem_inc(waited, 1)

                    def combine(hp, part):
                        toks, over = bass.ds(hp * GROUP, GROUP), [P, GROUP, D]
                        if part == 0:
                            steps[0] = 0
                            dve.wait_ge(x_again, hp * 16 + 16)
                            dve.tensor_copy(gsc[:, 0], mean[:, toks])
                            dve.tensor_copy(gsc[:, 1], rstd[:, toks])
                            then(hp, dve.tensor_copy(gsc[:, 2:4], weights[:, :, toks]))
                            for q in range(GROUP):
                                ins = dve.tensor_scalar(x_row[:, q], x_row[:, q], gsc[:, 0, q:q + 1],
                                                        gsc[:, 1, q:q + 1], ALU.subtract, ALU.mult)
                            then(hp, ins)
                        elif part in (1, 2):
                            if part == 1:
                                dve.wait_ge(gathered, hp * (16 * 2 * GROUP) + 16 * 2 * GROUP)
                            for q in range(GROUP):
                                ins = dve.scalar_tensor_tensor(out=x_row[:, q], in0=two_y[:, (part - 1) * GROUP + q],
                                                               scalar=gsc[:, 1 + part, q:q + 1], in1=x_row[:, q],
                                                               op0=ALU.mult, op1=ALU.add)
                            then(hp, ins)
                        elif part == 3:
                            for q in range(GROUP):
                                ins = dve.bn_stats(gstat[:, q], x_row[:, q])
                            then(hp, ins)
                            for q in range(GROUP):
                                ins = dve.bn_aggr(gmom[:, q], gstat[:, q])
                            then(hp, ins)
                            then(hp, dve.tensor_scalar(gvar[:, 0], gmom[:, :, 1], LN_EPS, None, ALU.add))
                        elif part == 4:
                            for ins in rsqrt_guess(dve, gvar[:, 0], gvar[:, 1], gvar[:, 2]):
                                then(hp, ins)
                        elif part in (5, 6, 7):
                            for ins in newton(dve, gvar[:, 0], gvar[:, 1], gvar[:, 2]):
                                then(hp, ins)
                        elif part == 8:
                            for q in range(GROUP):
                                ins = dve.tensor_scalar(x_row[:, q], x_row[:, q], gmom[:, q, 0:1],
                                                        gvar[:, 1, q:q + 1], ALU.subtract, ALU.mult)
                            then(hp, ins)
                        elif part == 9:
                            then(hp, dve.tensor_tensor(x_row[:], x_row[:], fgamma[:].unsqueeze(1).broadcast_to(over),
                                                       ALU.mult))
                        elif part == 10:
                            then(hp, dve.tensor_tensor(x_row[:], x_row[:], fbeta[:].unsqueeze(1).broadcast_to(over),
                                                       ALU.add))
                            group = acc[:, toks]
                            then(hp, dve.tensor_tensor(group, group, x_row[:], ALU.add))
                            assert steps[0] == COMBINE_STEPS

                    def add_y(hp, g, n, u):
                        t0, tiles = y_units[n]
                        src = misc_ps[bank_of(u, False)][:, 0:tiles * (D + 1)].rearrange("p (t d) -> p t d", t=tiles)
                        dve.wait_ge(misc_ready, n_misc(hp, u, False) + 1)
                        dve.reciprocal(rden[:, u % 2, 0:tiles], src[:, :, D]).then_inc(recip_done, 1)
                        dve.wait_ge(recip_done, n_y(hp, g, n) + 1)
                        for t in range(tiles):
                            row = acc[:, g // 2 * TILES + t0 + t]
                            ins = dve.scalar_tensor_tensor(out=row, in0=src[:, t, 0:D], scalar=rden[:, u % 2, t:t + 1],
                                                           in1=row, op0=ALU.mult, op1=ALU.add)
                        ins.then_inc(y_added, 1)

                    dve.sem_inc(pv_done, RING)
                    dve.sem_inc(y_added, 1)
                    w_lo(0)
                    dve.wait_ge(attn_consts, 1)
                    dve.wait_ge(small2_loaded, 32)
                    for o in first:
                        if o[0] == "project":
                            project(0, o[1], o[2], o[3], True)
                        elif o[0] == "max":
                            maximum(0, o[1], o[2])

                    def walk(hp, order, last):
                        for o in order:
                            kind, g, c, u = o
                            if kind == "max":
                                maximum(hp, g, c)
                            elif kind == "project":
                                project(hp, g, c, u, False)
                            elif kind == "weights":
                                w_lo(hp + 1)
                            elif kind == "y":
                                add_y(hp, g, c, u)
                            elif kind == "gather" and g == 0:
                                dve.tensor_copy(places[:].rearrange("p (n q) -> p n q", n=2),
                                                slots[:, :, bass.ds(hp * GROUP, GROUP)]).then_inc(group_taken, 1)
                            elif kind == "combine":
                                combine(hp, g)
                            elif kind == "low" and DIAG[c]:
                                half, j, q0 = chunks[c]
                                slot, width = (g * CH + c) % RING, (half + 1) * BANK - q0
                                dve.wait_ge(diag_masked, n_diag(hp, g, c) + 1)
                                dve.tensor_tensor(p_lo[:, slot, 0:width], probs[:, slot, 0:width],
                                                  p_hi[:, slot, 0:width].bitcast(F32),
                                                  ALU.subtract).then_inc(diag_split, 1)

                    run(dve, walk)

                @block.tensor
                def _(pe):
                    def misc_bank(hp, u, start):
                        units = first_units if start else body_units
                        if u < 2 and not start:
                            pe.wait_ge(y_added, n_y(hp, 0, 0) + 1)
                            pe.wait_ge(v_done, n_batch(hp, 0) * 2 + 2)
                            pe.wait_ge(shift_done, n_half(hp, 0, 0) + 1)
                        elif u >= 2:
                            kind, g, n = units[u - 2]
                            if kind == "project" and n < 4:
                                pe.wait_ge(lo_done, n_batch(hp, g) * 4 + (n + 1))
                            elif kind == "project":
                                pe.wait_ge(v_done, n_batch(hp, g) * 2 + (n - 3))
                            elif kind == "shift":
                                pe.wait_ge(shift_done, n_half(hp, g, n) + 1)
                            else:
                                pe.wait_ge(y_added, n_y(hp, g, n) + 2)
                        return misc_ps[bank_of(u, start)]

                    def project(hp, p, n, u, start):
                        toks = (p % BATCH) * SEQ
                        dst = misc_bank(hp, u, start)
                        if n < 4:
                            w = n // 2
                            cols = slice(toks + n % 2 * BANK, toks + (n % 2 + 1) * BANK)
                            if n == 0:
                                pe.wait_ge(wqk_split, hp + (p // BATCH + 1))
                            pe.matmul(dst[:], wqk_hi[:, w], nT_hi[:, cols], start=True, stop=False)
                            pe.matmul(dst[:], wqk_hi[:, w], nT_lo[:, cols], start=False, stop=False)
                            ins = pe.matmul(dst[:], wqk_lo[:, w], nT_hi[:, cols], start=False, stop=True)
                        else:
                            for q in range(GROUP):
                                t0 = toks + ((n - 4) * GROUP + q) * P
                                ins = pe.matmul(dst[:, q * P:(q + 1) * P], nT[:, t0:t0 + P], w_raw[:, 2],
                                                start=True, stop=True)
                        ins.then_inc(misc_ready, 1)

                    def max_scores_of(hp, g, t):
                        i, s = g // 2 % 2, g % 2
                        width = (t + 1) * P
                        if t == 0 and s == 0:
                            pe.wait_ge(copies_done, n_batch(hp, g // 2) * 64 + 64)
                            pe.wait_ge(lo_done, n_batch(hp, g // 2) * 4 + 4)
                        if t == 0:
                            pe.wait_ge(max_taken, n_max(hp, g, 0))
                        elif t >= 4:
                            pe.wait_ge(max_taken, n_max(hp, g, t))
                        elif t >= 2:
                            pe.wait_ge(max_taken, n_max(hp, g, t) - 1)
                        base = t % 2 * BANK if t < 4 else 0
                        for k0 in range(0, width, BANK):
                            k1 = min(k0 + BANK, width)
                            ins = pe.matmul(max_ps[:, base + k0:base + k1], q_a[i][s][:, t * P:(t + 1) * P],
                                            k_a[i][s][:, k0:k1], start=True, stop=True)
                        ins.then_inc(max_scores, 1)

                    def shifts(hp, g, half, u, start):
                        dst = misc_bank(hp, u, start)
                        pe.wait_ge(max_split, n_half(hp, g, half) + 1)
                        for q in range(GROUP):
                            ins = pe.transpose(dst[0:2, q * P:(q + 1) * P],
                                               shift[:, g % 2, half * GROUP + q, :].bitcast(F32), ident[:])
                        ins.then_inc(misc_ready, 1)

                    def score(hp, g, c):
                        half, j, q0 = chunks[c]
                        i, s = g // 2 % 2, g % 2
                        dst = score_ps[(g * CH + c) % 2][:, 0:(half + 1) * BANK - q0]
                        keys, qs = slice(j * P, (j + 1) * P), slice(q0, (half + 1) * BANK)
                        pe.wait_ge(probs_ready, n_chunk(hp, g, c) + 1)
                        if j == 0:
                            pe.wait_ge(shift_done, n_half(hp, g, half) + 1)
                        pe.matmul(dst, k_a[i][s][:, keys], q_a[i][s][:, qs], start=True, stop=False)
                        pe.matmul(dst, k_b[i][s][:, keys], q_b[i][s][:, qs], start=False,
                                  stop=True).then_inc(scores_ready, 1)

                    def values(hp, g, c):
                        half, j, q0 = chunks[c]
                        i, s = g // 2 % 2, g % 2
                        width = (half + 1) * BANK - q0
                        if DIAG[c]:
                            pe.wait_ge(diag_split, n_diag(hp, g, c) + 1)
                        else:
                            pe.wait_ge(full_split, n_full(hp, g, c) + 1)
                        if j == 0:
                            pe.wait_ge(heads_out[half], hp * G + (g + 1))
                        if c == 0:
                            pe.wait_ge(v_done, n_batch(hp, g // 2) * 2 + 2)
                        slot, cols = (g * CH + c) % RING, slice(q0, (half + 1) * BANK)
                        pe.matmul(head_ps[0:HEAD + 1, cols], v_hi[i][:, j, s], p_hi[:, slot, 0:width],
                                  start=(j == 0), stop=False)
                        pe.matmul(head_ps[0:HEAD, cols], v_lo[i][:, j, s], p_hi[:, slot, 0:width],
                                  start=False, stop=False)
                        pe.matmul(head_ps[0:HEAD + 1, cols], v_hi[i][:, j, s], p_lo[:, slot, 0:width],
                                  start=False, stop=c in LAST).then_inc(pv_done, 1)

                    def project_out(hp, g, n, u):
                        t0, tiles = y_units[n]
                        dst = misc_bank(hp, u, False)
                        if n == 0:
                            pe.wait_ge(heads_out[0], hp * G + (g + 2))
                            pe.wait_ge(heads_out[1], hp * G + (g + 2))
                            if g == 0:
                                pe.wait_ge(wout_loaded, hp * 16 + 16)
                        for t in range(tiles):
                            q0 = (t0 + t) * P
                            ins = pe.matmul(dst[:, t * (D + 1):(t + 1) * (D + 1)], heads[:, g % 2, q0:q0 + P],
                                            wo[:, g % 2], start=True, stop=True)
                        ins.then_inc(misc_ready, 1)

                    body_units = []
                    pe.wait_ge(attn_consts, 6)
                    for o in first:
                        if o[0] == "project":
                            project(0, o[1], o[2], o[3], True)
                        elif o[0] == "max":
                            max_scores_of(0, o[1], o[2])
                        else:
                            shifts(0, o[1], o[2], o[3], True)

                    def walk(hp, order, last):
                        body_units[:] = [o[:3] for o in order if o[-1] is not None]
                        for kind, g, c, u in order:
                            if kind == "score":
                                score(hp, g, c)
                            elif kind == "max":
                                max_scores_of(hp, g, c)
                            elif kind == "project":
                                project(hp, g, c, u, False)
                            elif kind == "shift":
                                shifts(hp, g, c, u, False)
                            elif kind == "pv":
                                values(hp, g, c)
                            elif kind == "y":
                                project_out(hp, g, c, u)

                    run(pe, walk)


_INS = ['L0_attn_x', 'L0_attn_gamma', 'L0_attn_w_qkv', 'L0_attn_w_out', 'L0_ffn_Wr', 'L0_ffn_br', 'L0_ffn_W1',
        'L0_ffn_b1', 'L0_ffn_W2', 'L0_ffn_b2', 'L0_ffn_gamma', 'L0_ffn_beta']
_OUTS = [((4, 1024, 128), 'float32')]


def kernel(**inputs):
    import numpy as _np
    import concourse.bacc as _bacc
    from concourse import mybir as _mybir
    from concourse.bass_utils import run_bass_kernel_spmd as _run

    nc = _bacc.Bacc("TRN2", target_bir_lowering=False, num_devices=1)
    arrays, args = {}, []
    for name in _INS:
        a = _np.ascontiguousarray(inputs[name])
        arrays[f"in_{name}_dram"] = a
        args.append(nc.dram_tensor(f"in_{name}_dram", a.shape, _mybir.dt.from_np(a.dtype), kind="ExternalInput").ap())
    for i, (shape, dtype) in enumerate(_OUTS):
        dt = _mybir.dt.from_np(_np.dtype(dtype))
        args.append(nc.dram_tensor(f"out_{i}_dram", shape, dt, kind="ExternalOutput").ap())
    attention_and_experts(nc, *args)
    r = _run(nc, [arrays], core_ids=[0])
    got = tuple(r.results[0][f"out_{i}_dram"] for i in range(len(_OUTS)))
    return got[0]
```

```python
from contextlib import ExitStack

import concourse.bass as bass
from concourse import mybir

ALU = mybir.AluOpType
ACT = mybir.ActivationFunctionType
AX_X = mybir.AxisListType.X
F32 = mybir.dt.float32
F32R = mybir.dt.float32r
BF16 = mybir.dt.bfloat16
I32 = mybir.dt.int32
U32 = mybir.dt.uint32

P = 128
BANK = 512
LN_EPS = 1e-5
RMS_EPS = 1e-12
TINY = 1e-30
MASKED = -1e30


def attention_and_experts(nc, x, attn_gamma, w_qkv, w_out, w_router, b_router,
                          w1, b1, w2, b2, ffn_gamma, ffn_beta, out):
    BATCH, SEQ, D = x.shape
    EXPERTS, FF, _ = w1.shape
    HEAD = 64
    HEADS = w_out.shape[0] // HEAD
    PAIRS = HEADS // 2
    TILES = SEQ // P
    ALL_TILES = BATCH * TILES
    HALVES = SEQ // BANK
    GROUP = BANK // P
    GROUPS = ALL_TILES // GROUP
    FT = FF // P
    SCALE = float(HEAD) ** -0.5
    assert D == P and SEQ == 2 * BANK and FF == BANK and 2 * HEAD == P

    x_tiles = x.rearrange("b (t p) d -> p (b t) d", p=P)
    out_tiles = out.rearrange("b (t p) d -> p (b t) d", p=P)

    with ExitStack() as whole:
        def sb(ctx, name, shape, dt=F32):
            return ctx.enter_context(nc.sbuf_tensor(name, shape, dt))

        def ps(ctx, name, shape, dt=F32):
            return ctx.enter_context(nc.psum_tensor(name, shape, dt))

        def sem(name):
            return whole.enter_context(nc.semaphore(name))

        acc = sb(whole, "acc", [P, ALL_TILES, D])
        nT = sb(whole, "nT", [P, ALL_TILES * P])
        nT_hi = sb(whole, "nT_hi", [P, ALL_TILES * P], F32R)
        nT_lo = sb(whole, "nT_lo", [P, ALL_TILES * P], F32R)
        ident = sb(whole, "ident", [P, P])

        mean = sb(whole, "mean", [P, ALL_TILES])
        rstd = sb(whole, "rstd", [P, ALL_TILES])
        slots = sb(whole, "slots", [P, 2, ALL_TILES], U32)
        weights = sb(whole, "weights", [P, 2, ALL_TILES])

        REGIONS = 2
        RT = ALL_TILES // REGIONS
        REGION = 2 * RT + EXPERTS - 1
        SORTED = REGIONS * REGION
        sorted_x = nc.dram_tensor("sorted_x", [SORTED * P, D], F32).ap()
        sorted_y = nc.dram_tensor("sorted_y", [SORTED * P, D], F32).ap()

        x_loaded = [sem(f"x_loaded{i}") for i in range(BATCH)]
        w1_loaded = [sem(f"w1_loaded{i}") for i in range(2)]
        w2_loaded = sem("w2_loaded")
        small_loaded = sem("small_loaded")
        set_up = sem("set_up")
        zeroed = sem("zeroed")
        dve_step = sem("dve_step")
        xn_ready = sem("xn_ready")
        nrm_ready = sem("nrm_ready")
        turned = sem("turned")
        act_read = sem("act_read")
        bank_free = [sem(f"bank_free{i}") for i in range(4)]
        logits_done = sem("logits_done")
        exp_asked = sem("exp_asked")
        exp_done = sem("exp_done")
        chosen_ready = sem("chosen_ready")
        counted = sem("counted")
        slots_ready = sem("slots_ready")
        scattered = [sem(f"scattered{i}") for i in range(REGIONS)]
        rows_loaded = [sem(f"rows_loaded{i}") for i in range(2)]
        rows_turned = sem("rows_turned")
        rows_hi = sem("rows_hi")
        rows_split = sem("rows_split")
        hidden_done = sem("hidden_done")
        hidden_copied = sem("hidden_copied")
        hidden_turned = sem("hidden_turned")
        relu_done = sem("relu_done")
        expert_out = sem("expert_out")
        expert_copied = sem("expert_copied")
        expert_stored = [sem(f"expert_stored{i}") for i in range(3)]
        waited = sem("waited")

        RSQRT_STEPS = 11

        def rsqrt_step(dve, n, v, y, t):
            if n == 0:
                return dve.tensor_scalar(t.bitcast(I32), v.bitcast(I32), 1, None, ALU.logical_shift_right)
            if n == 1:
                return dve.tensor_scalar(y.bitcast(I32), t.bitcast(I32), -1.0, float(0x5F3759DF), ALU.mult, ALU.add)
            if (n - 2) % 3 == 0:
                return dve.tensor_tensor(t, y, y, ALU.mult)
            if (n - 2) % 3 == 1:
                return dve.scalar_tensor_tensor(out=t, in0=t, scalar=-0.5, in1=v, op0=ALU.mult, op1=ALU.mult)
            return dve.scalar_tensor_tensor(out=y, in0=t, scalar=1.5, in1=y, op0=ALU.add, op1=ALU.mult)

        with ExitStack() as ph1:
            LOAD = 3
            RESULTS = 3
            assert REGION % LOAD == 0
            xn = sb(ph1, "xn", [P, ALL_TILES, D])
            nrm = sb(ph1, "nrm", [P, 2, TILES, D])
            w1_raw = sb(ph1, "w1_raw", [P, EXPERTS * FT, D])
            w2_raw = sb(ph1, "w2_raw", [P, EXPERTS, FF])
            w1T_hi = sb(ph1, "w1T_hi", [P, EXPERTS, FF], F32R)
            w1T_lo = sb(ph1, "w1T_lo", [P, EXPERTS, FF], F32R)
            w2T = sb(ph1, "w2T", [P, EXPERTS, FT, D])
            zeros = sb(ph1, "zeros", [P, SORTED * P // 13])
            wr_raw = sb(ph1, "wr_raw", [EXPERTS, D])
            b1_raw = sb(ph1, "b1_raw", [EXPERTS * FT, P])
            b2_all = sb(ph1, "b2_all", [P, EXPERTS, D])
            wrT = sb(ph1, "wrT", [P, EXPERTS])
            b1T = sb(ph1, "b1T", [P, EXPERTS * FT])
            br_all = sb(ph1, "br_all", [P, EXPERTS])
            agamma = sb(ph1, "agamma", [P, 1])
            ones = sb(ph1, "ones", [P, P])
            earlier = sb(ph1, "earlier", [P, P])
            before = sb(ph1, "before", [P, EXPERTS, EXPERTS])
            restart = sb(ph1, "restart", [P, EXPERTS, RT])
            tile_no = sb(ph1, "tile_no", [P, REGION])
            tile_no_int = sb(ph1, "tile_no_int", [P, REGION], I32)
            stats = sb(ph1, "stats", [P, TILES, 6])
            moments = sb(ph1, "moments", [P, TILES, 2])
            var2 = sb(ph1, "var2", [P, 2, TILES])
            root = sb(ph1, "root", [P, 2, TILES])
            tmp = sb(ph1, "tmp", [P, 2, TILES])
            nscale = sb(ph1, "nscale", [P, ALL_TILES])
            xnT = sb(ph1, "xnT", [P, 2, BANK])
            logit = sb(ph1, "logit", [P, RT, EXPERTS])
            more = sb(ph1, "more", [P, RT, EXPERTS, EXPERTS])
            same = sb(ph1, "same", [P, RT, EXPERTS, EXPERTS])
            rank = sb(ph1, "rank", [P, RT, EXPERTS])
            chosen = sb(ph1, "chosen", [P, RT, EXPERTS])
            pick = sb(ph1, "pick", [P, 2, RT, EXPERTS])
            prod = sb(ph1, "prod", [P, 2, RT, EXPERTS])
            two = sb(ph1, "two", [P, 2, RT])
            two_f = sb(ph1, "two_f", [P, 2, RT])
            gap = sb(ph1, "gap", [P, RT])
            upto = sb(ph1, "upto", [P, EXPERTS, RT])
            totals = sb(ph1, "totals", [P, EXPERTS, RT])
            tiles_int = sb(ph1, "tiles_int", [P, EXPERTS], I32)
            tiles_of = sb(ph1, "tiles_of", [P, EXPERTS])
            base = sb(ph1, "base", [P, EXPERTS])
            ends = sb(ph1, "ends", [P, EXPERTS])
            small = sb(ph1, "small", [P, EXPERTS, EXPERTS])
            slot = sb(ph1, "slot", [P, RT, EXPERTS])
            past = sb(ph1, "past", [P, REGION, EXPERTS])
            expert_f = sb(ph1, "expert_f", [P, REGION])
            tile_expert = sb(ph1, "tile_expert", [P, SORTED], I32)
            rowsT_hi = sb(ph1, "rowsT_hi", [P, 2, P], F32R)
            rowsT_lo = sb(ph1, "rowsT_lo", [P, 2, P], F32R)
            rows = w2_raw[:, 0:2].rearrange("p a b -> p (a b)")[:, 0:2 * LOAD * D].rearrange(
                "p (i q d) -> p i q d", i=2, q=LOAD)
            hidden = w1_raw[:, 0:2 * FT].rearrange("p (i f) d -> p i (f d)", i=2)
            hiddenT = w1_raw[:, 2 * FT:4 * FT].rearrange("p (i f) d -> p i f d", i=2)
            result = sb(ph1, "result", [P, RESULTS, D])
            bank = [ps(ph1, f"bank{i}", [P, BANK]) for i in range(4)]
            obank = [ps(ph1, f"obank{i}", [P, D]) for i in range(2)]
            lbank = ps(ph1, "lbank", [P, RT, EXPERTS])
            tbank = ps(ph1, "tbank", [P, BANK])
            turned_rows = [tbank[:, 0:P], lbank[:].rearrange("p t e -> p (t e)")]
            assert 2 * RT * EXPERTS <= BANK

            per_batch = TILES // GROUP
            units = [("wr", 0), ("b1", 0)]
            for b in range(2):
                for g in range(b * per_batch, (b + 1) * per_batch):
                    units += [("xn", g)]
            units += [("w1", e) for e in range(EXPERTS)] + [("w2", e) for e in range(EXPERTS)]
            for b in range(2):
                for g in range(b * per_batch, (b + 1) * per_batch):
                    units += [("n", g)]
            half_units = len(units)
            for b in range(2, BATCH):
                for g in range(b * per_batch, (b + 1) * per_batch):
                    units += [("xn", g)]
            for b in range(2, BATCH):
                for g in range(b * per_batch, (b + 1) * per_batch):
                    units += [("n", g)]
            reads, n = {}, 0
            for u, (kind, _) in enumerate(units):
                if kind in ("w1", "n"):
                    n += 1
                    reads[u] = n
            xn_units = [u for u, (kind, _) in enumerate(units) if kind == "xn"]

            def tbank_counts(n):
                return tbank[:, n * P:(n + 1) * P].rearrange("p (t e) -> p t e", e=EXPERTS)

            def freed(u):
                return u // 4 + 1

            UNROLL = 2 * LOAD
            FIRST = 3
            LOOPS = (SORTED - FIRST - 1) // UNROLL

            def expert_steps(eng, step):
                for j in range(FIRST):
                    step(j, j, None)
                with eng.Fori(0, LOOPS) as i:
                    for k in range(UNROLL):
                        step(i * UNROLL + (FIRST + k), FIRST + k, i)
                for j in range(FIRST + LOOPS * UNROLL, SORTED + 3):
                    step(j, j, None)

            def has(j, i, tile):
                return i is not None or 0 <= j + tile < SORTED

            def expert_of(eng, tile):
                return eng.value_load(tile_expert[0:1, bass.ds(tile, 1)], min_val=0, max_val=EXPERTS - 1)

            def times(k, i, ring):
                n = k // ring
                return n if i is None else i * (UNROLL // ring) + n

            with nc.Block() as block:

                @block.sync
                def _(sp):
                    for b in range(BATCH):
                        sp.dma_start(acc[:, b * TILES:(b + 1) * TILES],
                                     x_tiles[:, b * TILES:(b + 1) * TILES]).then_inc(x_loaded[b], 16)
                    sp.wait_ge(set_up, 1)
                    flat = sorted_x.rearrange("(p a) d -> p (a d)", p=P)
                    width = SORTED * P // 13
                    for i in range(13):
                        sp.dma_start(flat[:, i * width:(i + 1) * width], zeros[:]).then_inc(zeroed, 16)
                    src = sorted_x.rearrange("(j p) d -> p j d", p=P)

                    def load(m, slot):
                        sp.wait_ge(rows_turned, m * LOAD + 1)
                        sp.dma_start(rows[:, slot], src[:, bass.ds(m * LOAD, LOAD)]).then_inc(rows_loaded[slot], 16)

                    sp.wait_ge(turned, units.index(("w2", 1)) + 1)
                    loads = REGION // LOAD
                    for r in range(REGIONS):
                        sp.wait_ge(scattered[r], 16 * 2 * RT)
                        m = r * loads
                        if m % 2:
                            load(m, 1)
                            m += 1
                        rounds = ((r + 1) * loads - m) // 2
                        with sp.Fori(0, rounds) as i:
                            for slot in range(2):
                                load(i * 2 + (m + slot), slot)
                        if m + 2 * rounds < (r + 1) * loads:
                            load(m + 2 * rounds, 0)

                @block.gpsimd
                def _(pool):
                    pool.memset(zeros[:], 0.0).then_inc(set_up, 1)
                    pool.memset(ident[:], 1.0)
                    pool.memset(ones[:], 1.0)
                    pool.memset(earlier[:], 1.0)
                    pool.memset(restart[:], 1.0)
                    pool.iota(tile_no_int[:], [[1, REGION]], base=0, channel_multiplier=0)
                    pool.memset(before[:], 1.0).then_inc(set_up, 1)
                    pool.wait_ge(set_up, 2)
                    pool.memset(restart[:, :, 0:1], 0.0)
                    pool.affine_select(out=ident[:], in_=ident[:], pattern=[[1, P]], compare_op=ALU.is_equal,
                                       fill=0.0, base=0, channel_multiplier=-1).then_inc(set_up, 1)
                    pool.affine_select(out=earlier[:], in_=earlier[:], pattern=[[1, P]], compare_op=ALU.is_gt,
                                       fill=0.0, base=0, channel_multiplier=-1).then_inc(set_up, 1)
                    pool.affine_select(out=before[:], in_=before[:], pattern=[[1, EXPERTS], [-1, EXPERTS]],
                                       compare_op=ALU.is_gt, fill=0.0, base=0,
                                       channel_multiplier=0).then_inc(set_up, 1)
                    pool.tensor_copy(tile_no[:], tile_no_int[:]).then_inc(set_up, 1)

                    pool.wait_ge(zeroed, 16 * 13)
                    for r in range(REGIONS):
                        pool.wait_ge(slots_ready, r + 1)
                        for t in range(r * RT, (r + 1) * RT):
                            for n in range(2):
                                pool.indirect_dma_start(
                                    sorted_x, bass.IndirectOffsetOnAxis(ap=slots[:, n, t:t + 1], axis=0),
                                    xn[:, t], None).then_inc(scattered[r], 16)

                @block.scalar
                def _(act):
                    w1_src = w1.rearrange("e (f p) d -> p (e f) d", p=P)
                    with nc.allow_non_contiguous_dma(reason="one column of gamma"):
                        act.dma_start(agamma[:], attn_gamma.rearrange("(p a) -> p a", a=1)).then_inc(small_loaded, 16)
                    act.dma_start(wr_raw[:], w_router).then_inc(small_loaded, 16)
                    act.dma_start(b1_raw[:], b1.rearrange("e (f p) -> (e f) p", p=P)).then_inc(small_loaded, 16)
                    act.dma_start(br_all[:], b_router.partition_broadcast(P)).then_inc(small_loaded, 16)
                    half = EXPERTS * FT // 2
                    for i in range(2):
                        act.dma_start(w1_raw[:, i * half:(i + 1) * half],
                                      w1_src[:, i * half:(i + 1) * half]).then_inc(w1_loaded[i], 16)
                    act.dma_start(w2_raw[:], w2.rearrange("e d f -> d e f")).then_inc(w2_loaded, 16)
                    act.dma_start(b2_all[:], b2.partition_broadcast(P)).then_inc(small_loaded, 16)

                    def normed(b):
                        act.wait_ge(xn_ready, b + 1)
                        if b >= 2:
                            act.wait_ge(turned, units.index(("n", (b - 1) * per_batch - 1)) + 1)
                        for t in range(TILES):
                            ins = act.activation(nrm[:, b % 2, t], xn[:, b * TILES + t], ACT.Copy,
                                                 scale=nscale[:, b * TILES + t:b * TILES + t + 1])
                        ins.then_inc(nrm_ready, 1)

                    def evacuate(u):
                        kind, n = units[u]
                        src = bank[u % 4]
                        act.wait_ge(turned, u + 1)
                        cols = slice(n * BANK, (n + 1) * BANK)
                        if kind == "w1":
                            act.activation(w1T_hi[:, n], src[:], ACT.Copy).then_inc(act_read, 1)
                        elif kind == "n":
                            act.activation(nT[:, cols], src[:], ACT.Copy, scale=agamma[:, 0:1])
                            act.activation(nT_hi[:, cols], src[:], ACT.Copy,
                                           scale=agamma[:, 0:1]).then_inc(act_read, 1)
                        elif kind == "wr":
                            act.activation(wrT[:], src[:, 0:EXPERTS], ACT.Copy).then_inc(bank_free[u % 4], 1)
                        elif kind == "xn":
                            if n >= 2:
                                act.wait_ge(logits_done, n - 1)
                            act.activation(xnT[:, n % 2], src[:], ACT.Copy).then_inc(bank_free[u % 4], 1)
                        elif kind == "w2":
                            act.activation(w2T[:, n].rearrange("p f d -> p (f d)"), src[:],
                                           ACT.Copy).then_inc(bank_free[u % 4], 1)
                        elif kind == "b1":
                            act.activation(b1T[:], src[:, 0:EXPERTS * FT], ACT.Copy).then_inc(bank_free[u % 4], 1)

                    def exponentials(r):
                        act.wait_ge(exp_asked, r + 1)
                        act.activation(two[:, 1], gap[:], ACT.Exp).then_inc(exp_done, 1)

                    act.wait_ge(small_loaded, 16 * 5)
                    for u in range(half_units):
                        if u == units.index(("w1", 0)):
                            for b in range(2):
                                normed(b)
                        if u == units.index(("w2", 0)):
                            exponentials(0)
                        evacuate(u)
                    for u in range(half_units, len(units)):
                        if u == half_units + 4:
                            for b in range(2, BATCH):
                                normed(b)
                        evacuate(u)
                    exponentials(1)

                    def step(j, k, i):
                        if has(j, i, -1):
                            e = expert_of(act, j - 1)
                        if k == 0 and i is None:
                            rows_to_hi(0, 0)
                        if has(j, i, 1):
                            rows_to_hi(j + 1, k + 1)
                        if has(j, i, -1):
                            act.wait_ge(hidden_turned, j)
                            for f in range(FT):
                                ins = act.activation(hiddenT[:, (k - 1) % 2, f],
                                                     bank[2 + (k - 1) % 2][:, f * P:(f + 1) * P], ACT.Relu,
                                                     bias=b1T[:, bass.ds(e * FT + f, 1)])
                            ins.then_inc(relu_done, 1)
                        if has(j, i, -3):
                            act.wait_ge(expert_copied, j - 2 + 4)
                            act.dma_start(sorted_y[bass.ds((j - 3) * P, P), :],
                                          result[:, k % RESULTS]).then_inc(expert_stored[k % RESULTS], 16)

                    def rows_to_hi(j, k):
                        act.wait_ge(rows_turned, j + 1 + (LOAD + 1))
                        act.activation(rowsT_hi[:, k % 2], turned_rows[k % 2], ACT.Copy).then_inc(rows_hi, 1)

                    act.wait_ge(set_up, 7)
                    act.sem_inc(waited, 1)
                    expert_steps(act, step)
                    for n in range(RESULTS):
                        act.wait_ge(expert_stored[n], 16 * (1 + len(range(n, SORTED, RESULTS))))

                @block.vector
                def _(dve):
                    steps = [0]

                    def then(ins):
                        steps[0] += 1
                        ins.then_inc(dve_step, 1)
                        dve.wait_ge(dve_step, steps[0])

                    dve.sem_inc(rows_turned, LOAD + 1)
                    dve.sem_inc(expert_copied, 4)
                    for n in range(RESULTS):
                        dve.sem_inc(expert_stored[n], 16)

                    def layernorm(b):
                        tiles = slice(b * TILES, (b + 1) * TILES)
                        dve.wait_ge(x_loaded[b], 16)
                        for t in range(TILES):
                            ins = dve.bn_stats(stats[:, t], acc[:, b * TILES + t])
                        then(ins)
                        for t in range(TILES):
                            ins = dve.bn_aggr(moments[:, t], stats[:, t])
                        then(ins)
                        dve.tensor_scalar(mean[:, tiles], moments[:, :, 0], 1.0, None, ALU.mult)
                        dve.tensor_scalar(var2[:, 0], moments[:, :, 1], LN_EPS, None, ALU.add)
                        then(dve.tensor_scalar(var2[:, 1], moments[:, :, 1], float(D), TINY, ALU.mult, ALU.max))
                        for n in range(RSQRT_STEPS):
                            then(rsqrt_step(dve, n, var2[:], root[:], tmp[:]))
                        dve.tensor_scalar(rstd[:, tiles], root[:, 0], 1.0, None, ALU.mult)
                        then(dve.tensor_tensor(tmp[:, 0], root[:, 1], var2[:, 1], ALU.mult))
                        then(dve.tensor_tensor(tmp[:, 0], tmp[:, 0], root[:, 0], ALU.mult))
                        then(dve.tensor_scalar(tmp[:, 0], tmp[:, 0], RMS_EPS, None, ALU.max))
                        then(dve.reciprocal(tmp[:, 1], tmp[:, 0]))
                        then(dve.tensor_scalar(nscale[:, tiles], tmp[:, 1], float(D) ** 0.5, None, ALU.mult))
                        for t in range(b * TILES, (b + 1) * TILES):
                            ins = dve.tensor_scalar(xn[:, t], acc[:, t], mean[:, t:t + 1], rstd[:, t:t + 1],
                                                    ALU.subtract, ALU.mult)
                        ins.then_inc(xn_ready, 1)

                    def lower(u):
                        kind, n = units[u]
                        src = bank[u % 4]
                        if u not in reads:
                            return
                        dve.wait_ge(act_read, reads[u])
                        if kind == "w1":
                            dve.tensor_tensor(w1T_lo[:, n], src[:], w1T_hi[:, n].bitcast(F32),
                                              ALU.subtract).then_inc(bank_free[u % 4], 1)
                        else:
                            cols = slice(n * BANK, (n + 1) * BANK)
                            dve.scalar_tensor_tensor(out=nT_lo[:, cols], in0=src[:], scalar=agamma[:, 0:1],
                                                     in1=nT_hi[:, cols].bitcast(F32), op0=ALU.mult,
                                                     op1=ALU.subtract).then_inc(bank_free[u % 4], 1)

                    def router(r):
                        over = [P, RT, EXPERTS]
                        shape4 = [P, RT, EXPERTS, EXPERTS]
                        dve.wait_ge(logits_done, (r + 1) * RT // GROUP)
                        then(dve.tensor_tensor(logit[:], lbank[:], br_all[:].unsqueeze(1).broadcast_to(over),
                                               ALU.add))
                        mine = logit[:].unsqueeze(3).broadcast_to(shape4)
                        other = logit[:].unsqueeze(2).broadcast_to(shape4)
                        dve.tensor_tensor(more[:], other, mine, ALU.is_gt)
                        then(dve.tensor_tensor(same[:], other, mine, ALU.is_equal))
                        then(dve.tensor_tensor(same[:], same[:], before[:].unsqueeze(1).broadcast_to(shape4),
                                               ALU.mult))
                        then(dve.tensor_tensor(more[:], more[:], same[:], ALU.add))
                        then(dve.tensor_reduce(rank[:], more[:], AX_X, ALU.add))
                        dve.tensor_scalar(chosen[:], rank[:], 1.5, None, ALU.is_lt).then_inc(chosen_ready, 1)
                        dve.tensor_scalar(pick[:, 0], rank[:], 0.0, None, ALU.is_equal)
                        then(dve.tensor_scalar(pick[:, 1], rank[:], 1.0, None, ALU.is_equal))
                        then(dve.tensor_tensor(prod[:], pick[:], logit[:].unsqueeze(1).broadcast_to(
                            [P, 2, RT, EXPERTS]), ALU.mult))
                        then(dve.tensor_reduce(two[:], prod[:], AX_X, ALU.add))
                        dve.tensor_tensor(gap[:], two[:, 1], two[:, 0], ALU.subtract).then_inc(exp_asked, 1)

                    def places(r):
                        toks = slice(r * RT, (r + 1) * RT)
                        dve.wait_ge(counted, r + 1)
                        dve.tensor_copy(totals[:], tbank_counts(1).rearrange("p t e -> p e t"))
                        then(dve.tensor_copy(slot[:], tbank_counts(0)))
                        then(dve.tensor_tensor_scan(upto[:].rearrange("p e t -> p (e t)"),
                                                    restart[:].rearrange("p e t -> p (e t)"),
                                                    totals[:].rearrange("p e t -> p (e t)"),
                                                    0.0, ALU.mult, ALU.add))
                        then(dve.tensor_scalar(tiles_int[:], upto[:, :, RT - 1], 1.0 / P,
                                               (P - 1) / P - 0.5 + 0.5 / P, ALU.mult, ALU.add))
                        then(dve.tensor_copy(tiles_of[:], tiles_int[:]))
                        then(dve.tensor_tensor(small[:], before[:], tiles_of[:].unsqueeze(1).broadcast_to(
                            [P, EXPERTS, EXPERTS]), ALU.mult))
                        then(dve.tensor_reduce(base[:], small[:], AX_X, ALU.add))
                        then(dve.tensor_tensor(ends[:], base[:], tiles_of[:], ALU.add))
                        then(dve.tensor_scalar(base[:], base[:], float(P), float(r * REGION * P), ALU.mult, ALU.add))
                        then(dve.tensor_tensor(upto[:], upto[:], totals[:], ALU.subtract))
                        then(dve.tensor_tensor(upto[:], upto[:], base[:].unsqueeze(2).broadcast_to(
                            [P, EXPERTS, RT]), ALU.add))
                        then(dve.tensor_tensor(slot[:], slot[:], upto[:].rearrange("p e t -> p t e"), ALU.add))
                        then(dve.tensor_tensor(prod[:], pick[:], slot[:].unsqueeze(1).broadcast_to(
                            [P, 2, RT, EXPERTS]), ALU.mult))
                        then(dve.tensor_reduce(two_f[:], prod[:], AX_X, ALU.add))
                        dve.tensor_copy(slots[:, :, toks], two_f[:]).then_inc(slots_ready, 1)
                        over = [P, REGION, EXPERTS]
                        dve.wait_ge(set_up, 6)
                        then(dve.tensor_tensor(past[:], tile_no[:].unsqueeze(2).broadcast_to(over),
                                               ends[:].unsqueeze(1).broadcast_to(over), ALU.is_ge))
                        then(dve.tensor_reduce(expert_f[:], past[:], AX_X, ALU.add))
                        then(dve.tensor_scalar(tile_expert[:, r * REGION:(r + 1) * REGION], expert_f[:],
                                               float(EXPERTS - 1), None, ALU.min))
                        dve.wait_ge(exp_done, r + 1)
                        then(dve.tensor_scalar(gap[:], two[:, 1], 1.0, None, ALU.add))
                        then(dve.reciprocal(weights[:, 0, toks], gap[:]))
                        then(dve.tensor_tensor(weights[:, 1, toks], two[:, 1], weights[:, 0, toks], ALU.mult))

                    dve.wait_ge(small_loaded, 16 * 5)
                    layernorm(0)
                    layernorm(1)
                    dve.wait_ge(set_up, 5)
                    router(0)
                    for u in range(units.index(("w1", 4))):
                        lower(u)
                    places(0)
                    layernorm(2)
                    for u in range(units.index(("w1", 4)), half_units):
                        lower(u)
                        if u == units.index(("w1", 5)):
                            layernorm(3)
                    for u in range(half_units, half_units + 4):
                        lower(u)
                    router(1)
                    places(1)
                    dve.sem_inc(set_up, 1)
                    for u in range(half_units + 4, len(units)):
                        lower(u)

                    def rows_to_lo(j, k):
                        dve.wait_ge(rows_hi, j + 1)
                        dve.tensor_tensor(rowsT_lo[:, k % 2], turned_rows[k % 2], rowsT_hi[:, k % 2].bitcast(F32),
                                          ALU.subtract).then_inc(rows_split, 1)

                    def step(j, k, i):
                        if has(j, i, -2):
                            e = expert_of(dve, j - 2)
                        if k == 0 and i is None:
                            rows_to_lo(0, 0)
                        if has(j, i, 1):
                            rows_to_lo(j + 1, k + 1)
                        if has(j, i, 0):
                            dve.wait_ge(hidden_done, j + 1)
                            dve.tensor_copy(hidden[:, k % 2], bank[k % 2][:]).then_inc(hidden_copied, 1)
                        if has(j, i, -2):
                            dve.wait_ge(expert_stored[(k - 2) % RESULTS], times(k - 2, i, RESULTS) * 16 + 16)
                            dve.wait_ge(expert_out, j - 1)
                            dve.tensor_tensor(result[:, (k - 2) % RESULTS], obank[k % 2][:],
                                              b2_all[:, bass.ds(e, 1)].rearrange("p e d -> p (e d)"),
                                              ALU.add).then_inc(expert_copied, 1)

                    expert_steps(dve, step)

                @block.tensor
                def _(pe):
                    def turn(u):
                        kind, n = units[u]
                        if u >= 4:
                            pe.wait_ge(bank_free[u % 4], freed(u - 4))
                        dst = bank[u % 4]
                        if kind == "w1":
                            if n % (EXPERTS // 2) == 0:
                                pe.wait_ge(w1_loaded[n // (EXPERTS // 2)], 16)
                            for f in range(FT):
                                ins = pe.transpose(dst[:, f * P:(f + 1) * P], w1_raw[:, n * FT + f], ident[:])
                        elif kind == "w2":
                            if n == 0:
                                pe.wait_ge(w2_loaded, 16)
                            for f in range(FT):
                                ins = pe.transpose(dst[:, f * P:(f + 1) * P], w2_raw[:, n, f * P:(f + 1) * P],
                                                   ident[:])
                        elif kind == "wr":
                            ins = pe.transpose(dst[:, 0:EXPERTS], wr_raw[:], ident[0:EXPERTS, 0:EXPERTS])
                        elif kind == "b1":
                            ins = pe.transpose(dst[:, 0:EXPERTS * FT], b1_raw[:],
                                               ident[0:EXPERTS * FT, 0:EXPERTS * FT])
                        else:
                            b = n // per_batch
                            pe.wait_ge(xn_ready if kind == "xn" else nrm_ready, b + 1)
                            for q in range(GROUP):
                                t = n * GROUP + q
                                src = xn[:, t] if kind == "xn" else nrm[:, b % 2, t % TILES]
                                ins = pe.transpose(dst[:, q * P:(q + 1) * P], src, ident[:])
                        ins.then_inc(turned, 1)

                    def logits(g):
                        u = units.index(("xn", g))
                        pe.wait_ge(bank_free[u % 4], freed(u))
                        if g == RT // GROUP:
                            pe.wait_ge(chosen_ready, 1)
                        for q in range(GROUP):
                            ins = pe.matmul(lbank[:, (g * GROUP + q) % RT], xnT[:, g % 2, q * P:(q + 1) * P], wrT[:],
                                            start=True, stop=True)
                        ins.then_inc(logits_done, 1)

                    def count(r):
                        pe.wait_ge(chosen_ready, r + 1)
                        pe.matmul(tbank_counts(0), earlier[:], chosen[:], start=True, stop=True)
                        pe.matmul(tbank_counts(1), ones[:], chosen[:], start=True, stop=True).then_inc(counted, 1)

                    pe.wait_ge(small_loaded, 16 * 5)
                    pe.wait_ge(set_up, 5)
                    groups = RT // GROUP
                    for u in range(2 + groups):
                        turn(u)
                        if u >= 3:
                            logits(u - 3)
                    logits(groups - 1)
                    for u in range(2 + groups, half_units):
                        if u == units.index(("w1", 4)):
                            count(0)
                        turn(u)
                    for g in range(groups):
                        turn(half_units + g)
                        if g:
                            logits(groups + g - 1)
                    logits(2 * groups - 1)
                    for u in range(half_units + groups, len(units)):
                        if u == half_units + groups + 2:
                            pe.wait_ge(slots_ready, 1)
                            count(1)
                        turn(u)
                    for u in range(len(units) - 4, len(units)):
                        pe.wait_ge(bank_free[u % 4], freed(u))
                    pe.wait_ge(set_up, 7)
                    pe.sem_inc(waited, 1)

                    tile_experts = {}

                    def turn_rows(j, k, i):
                        slot = k // LOAD % 2
                        if k % LOAD == 0:
                            pe.wait_ge(rows_loaded[slot], times(k, i, 2 * LOAD) * 16 + 16)
                        pe.transpose(turned_rows[k % 2], rows[:, slot, k % LOAD], ident[:]).then_inc(rows_turned, 1)

                    def step(j, k, i):
                        if has(j, i, 0):
                            tile_experts[k] = expert_of(pe, j)
                            e_in = tile_experts[k]
                        if has(j, i, -2):
                            inside = i is not None and k >= FIRST + 2
                            e_out = tile_experts[k - 2] if inside else expert_of(pe, j - 2)
                        if k == 0 and i is None:
                            turn_rows(0, 0, None)
                        if has(j, i, 1):
                            turn_rows(j + 1, k + 1, i)
                        if has(j, i, -1):
                            pe.wait_ge(hidden_copied, j)
                            for f in range(FT):
                                ins = pe.transpose(bank[2 + (k - 1) % 2][:, f * P:(f + 1) * P],
                                                   hidden[:, (k - 1) % 2, f * P:(f + 1) * P], ident[:])
                            ins.then_inc(hidden_turned, 1)
                        if has(j, i, 0):
                            pe.wait_ge(rows_split, j + 1)
                            w_hi = w1T_hi[:, bass.ds(e_in, 1)].rearrange("p e f -> p (e f)")
                            w_lo = w1T_lo[:, bass.ds(e_in, 1)].rearrange("p e f -> p (e f)")
                            pe.matmul(bank[k % 2][:], rowsT_hi[:, k % 2], w_hi, start=True, stop=False)
                            pe.matmul(bank[k % 2][:], rowsT_hi[:, k % 2], w_lo, start=False, stop=False)
                            pe.matmul(bank[k % 2][:], rowsT_lo[:, k % 2], w_hi, start=False,
                                      stop=True).then_inc(hidden_done, 1)
                        if has(j, i, -2):
                            pe.wait_ge(relu_done, j - 1)
                            pe.wait_ge(expert_copied, j - 3 + 4)
                            for f in range(FT):
                                ins = pe.matmul(obank[k % 2][:], hiddenT[:, (k - 2) % 2, f],
                                                w2T[:, bass.ds(e_out, 1), f].rearrange("p e d -> p (e d)"),
                                                start=(f == 0), stop=(f == FT - 1))
                            ins.then_inc(expert_out, 1)

                    expert_steps(pe, step)

        qkv_loaded = sem("qkv_loaded")
        wout_loaded = sem("wout_loaded")
        wqk_hi_done = sem("wqk_hi_done")
        wqk_split = sem("wqk_split")
        mask_zeroed = sem("mask_zeroed")
        attn_consts = sem("attn_consts")
        max_scores = sem("max_scores")
        max_taken = sem("max_taken")
        max_split = sem("max_split")
        max_step = sem("max_step")
        misc_ready = sem("misc_ready")
        hi_done = sem("hi_done")
        lo_done = sem("lo_done")
        v_hi_done = sem("v_hi_done")
        v_done = sem("v_done")
        pool_split = sem("pool_split")
        dve_split = sem("dve_split")
        copies_done = sem("copies_done")
        shift_done = sem("shift_done")
        scores_ready = sem("scores_ready")
        probs_ready = sem("probs_ready")
        diag_masked = sem("diag_masked")
        pv_done = sem("pv_done")
        heads_out = [sem(f"heads_out{i}") for i in range(2)]
        recip_done = sem("recip_done")
        y_added = sem("y_added")
        stored = sem("stored")
        small2_loaded = sem("small2_loaded")
        group_taken = sem("group_taken")
        gathered = sem("gathered")
        x_again = sem("x_again")
        comb_step = sem("comb_step")

        with ExitStack() as ph2:
            q_a = [[sb(ph2, f"q_a{i}{s}", [P, SEQ], F32R) for s in range(2)] for i in range(2)]
            k_a = [[sb(ph2, f"k_a{i}{s}", [P, SEQ], F32R) for s in range(2)] for i in range(2)]
            q_b = [[sb(ph2, f"q_b{i}{s}", [HEAD + 2, SEQ], F32R) for s in range(2)] for i in range(2)]
            k_b = [[sb(ph2, f"k_b{i}{s}", [HEAD + 2, SEQ], F32R) for s in range(2)] for i in range(2)]
            v_hi = [sb(ph2, f"v_hi{i}", [P, TILES, 2, HEAD + 1], F32R) for i in range(2)]
            v_lo = [sb(ph2, f"v_lo{i}", [P, TILES, 2, HEAD], F32R) for i in range(2)]
            RING = 4
            probs = sb(ph2, "probs", [P, RING, BANK])
            p_hi = sb(ph2, "p_hi", [P, RING, BANK], F32R)
            p_lo = sb(ph2, "p_lo", [P, RING, BANK], F32R)
            heads = sb(ph2, "heads", [HEAD + 1, 2, SEQ])
            w_raw = sb(ph2, "w_raw", [P, 3, P])
            wqk_hi = sb(ph2, "wqk_hi", [P, 2, P], F32R)
            wqk_lo = sb(ph2, "wqk_lo", [P, 2, P], F32R)
            wo = sb(ph2, "wo", [HEAD + 1, 2, D + 1])
            mask = sb(ph2, "mask", [P, SEQ])
            unread = sb(ph2, "unread", [P, 2, BANK], BF16)
            row_max = sb(ph2, "row_max", [P, 2, TILES])
            shift = sb(ph2, "shift", [P, 2, TILES, 2], F32R)
            rden = sb(ph2, "rden", [P, 2, 4])
            fgamma = sb(ph2, "fgamma", [P, D])
            fbeta = sb(ph2, "fbeta", [P, D])
            places = sb(ph2, "places", [P, 2 * GROUP], U32)
            two_y = sb(ph2, "two_y", [P, 2 * GROUP, D])
            x_row = sb(ph2, "x_row", [P, GROUP, D])
            gstat = sb(ph2, "gstat", [P, GROUP, 6])
            gmom = sb(ph2, "gmom", [P, GROUP, 2])
            gvar = sb(ph2, "gvar", [P, 3, GROUP])
            gsc = sb(ph2, "gsc", [P, 4, GROUP])
            max_ps = ps(ph2, "max_ps", [P, 2, BANK])
            score_ps = [ps(ph2, f"score_ps{i}", [P, BANK]) for i in range(2)]
            head_ps = ps(ph2, "head_ps", [P, SEQ])
            misc_ps = [ps(ph2, f"misc_ps{i}", [P, BANK]) for i in range(2)]

            chunks = [(half, j, max(half * BANK, j * P))
                      for half, keys in ((0, (0, 3, 1, 2)), (1, (0, 7, 1, 6, 2, 5, 4, 3))) for j in keys]
            LAST = [3, 11]
            CH = len(chunks)
            DIAG = [q0 == j * P for _, j, q0 in chunks]
            WIDTH = [(half + 1) * BANK - q0 for half, _, q0 in chunks]
            BY_DVE = [DIAG[c] and WIDTH[c] > 2 * P for c in range(CH)]
            LAG = 3
            G = BATCH * 2
            max_parts = [(0, 0), (1, 0), (2, 0), (3, 0), (4, 0), (5, 0), (4, BANK), (6, 0), (5, BANK), (7, 0),
                         (6, BANK), (7, BANK)]
            MAX_AT = list(range(CH))
            assert len(max_parts) == CH and CH % 2 == 0
            PROJECT_AT = [{0: 0, 1: 1, 3: 2, 5: 3}, {1: 4, 5: 5}]
            GATHER_AT = [(1, c) for c in (6, 7, 8, 9, 10, 11)] + [(2, c) for c in (1, 3, 5)]
            COMBINE_AT = [(g, c) for g in (3, 4, 5) for c in (0, 2, 3, 6, 7, 10, 11)][:10 + RSQRT_STEPS]
            COMBINE_STEPS = 11 + RSQRT_STEPS
            Y_AT = [4, 7, 9]
            y_units = [(0, 3), (3, 3), (6, 2)]

            CUT = 11
            MISC_KINDS = ("project", "shift", "y")

            def beside(g, c, last):
                order, at = [], g * CH + c
                final = G if last else 2 * G
                if g < final:
                    order.append(("score", g, c))
                if at >= LAG - 1 and (at - LAG + 1) // CH < final:
                    order.append(("low", (at - LAG + 1) // CH, (at - LAG + 1) % CH))
                if g + 1 < final and c in MAX_AT:
                    order.append(("max", g + 1, MAX_AT.index(c)))
                for kind, at0 in (("max_hi", 0), ("max_lo", 1)):
                    if g < final and c == at0:
                        order.append((kind, g, 1))
                    if g + 1 < final and c == at0 + 4:
                        order.append((kind, g + 1, 0))
                if c in PROJECT_AT[g % 2] and (g // 2 + 1) * 2 < final:
                    order.append(("project", g // 2 + 1, PROJECT_AT[g % 2][c]))
                if g and g < final and c in Y_AT:
                    order.append(("y", g - 1, Y_AT.index(c)))
                    order.append(("add", g - 1, Y_AT.index(c)))
                if g + 1 < final and c == 8:
                    order.append(("shift", g + 1, 0))
                if g < final and c == 2:
                    order.append(("shift", g, 1))
                if (g, c) in GATHER_AT:
                    order.append(("gather", GATHER_AT.index((g, c)), 0))
                if (g, c) in COMBINE_AT:
                    order.append(("combine", COMBINE_AT.index((g, c)), 0))
                if g == G - 3 and c == 10 and not last:
                    order.append(("weights", 0, 0))
                if at >= LAG:
                    order.append(("pv", (at - LAG) // CH, (at - LAG) % CH))
                return order

            def numbered(order, n):
                out_, outputs = [], {}
                for o in order:
                    if o[0] in MISC_KINDS:
                        outputs[o[1:]] = n if o[0] == "y" else None
                        out_.append((*o, n))
                        n += 1
                    else:
                        out_.append((*o, outputs[o[1:]] if o[0] == "add" else None))
                return out_

            def misc_units(order):
                return [o[:3] for o in order if o[0] in MISC_KINDS]

            before_loop = ([("project", 0, n) for n in range(6)] + [("max", 0, m) for m in range(len(max_parts))]
                           + [("max_hi", 0, 0), ("max_lo", 0, 0), ("shift", 0, 0)])
            for c in range(CUT):
                before_loop += beside(0, c, False)
            before_loop = numbered(before_loop, 0)
            first_units = misc_units(before_loop)
            MISC0 = len(first_units)

            def plan(last):
                order = []
                for at in range(CUT, G * CH + (LAG if last else CUT)):
                    order += beside(at // CH, at % CH, last)
                if last:
                    order += [(kind, G - 1, n) for n in range(len(y_units)) for kind in ("y", "add")]
                return numbered(order, MISC0)

            MISC = len(misc_units(plan(False)))
            assert MISC % 2 == 0

            def n_max(hp, g, m):
                return hp * (G * len(max_parts)) + (g * len(max_parts) + m)

            def n_chunk(hp, g, c):
                return hp * (G * CH) + (g * CH + c)

            def n_diag(hp, g, c):
                return hp * (G * sum(DIAG)) + (g * sum(DIAG) + sum(DIAG[:c]))

            def n_dve(hp, g, c):
                return hp * (G * sum(BY_DVE)) + (g * sum(BY_DVE) + sum(BY_DVE[:c]))

            def n_pool(hp, g, c):
                return hp * (G * (CH - sum(BY_DVE))) + (g * (CH - sum(BY_DVE)) + c - sum(BY_DVE[:c]))

            def n_misc(hp, u):
                return hp * MISC + u

            def n_half(hp, g, half):
                return hp * (G * 2) + (g * 2 + half)

            def n_y(hp, g, n):
                return hp * (G * len(y_units)) + (g * len(y_units) + n)

            def n_batch(hp, p):
                return hp * BATCH + p

            def run(walk, eng):
                walk(0, before_loop, False)
                with eng.Fori(0, PAIRS - 1) as hp:
                    walk(hp, plan(False), False)
                walk(PAIRS - 1, plan(True), True)

            with nc.Block() as block:

                @block.sync
                def _(sp):
                    def weights(hp):
                        src = w_qkv.rearrange("d (s h c) -> d s h c", s=3, c=P)
                        sp.dma_start(w_raw[:], src[:, :, bass.ds(hp, 1)].rearrange("d s h c -> d (s h) c")
                                     ).then_inc(qkv_loaded, 16)

                    def out_weights(hp):
                        src = w_out.rearrange("(h s c) d -> c h s d", s=2, c=HEAD)
                        sp.dma_start(wo[0:HEAD, :, 0:D], src[:, bass.ds(hp, 1)].rearrange("c h s d -> c (h s) d")
                                     ).then_inc(wout_loaded, 16)

                    def copies(hp, p):
                        i = p % 2
                        sp.wait_ge(hi_done, n_batch(hp, p) * 8 + 8)
                        for s in range(2):
                            k_hi, q_hi = k_a[i][s][0:HEAD, :].bitcast(F32), q_a[i][s][0:HEAD, :].bitcast(F32)
                            sp.dma_start(k_a[i][s][HEAD:P, :].bitcast(F32), k_hi).then_inc(copies_done, 16)
                            sp.dma_start(q_b[i][s][0:HEAD, :].bitcast(F32), q_hi).then_inc(copies_done, 16)

                    weights(0)
                    sp.dma_start(fgamma[:], ffn_gamma.partition_broadcast(P)).then_inc(small2_loaded, 16)
                    sp.dma_start(fbeta[:], ffn_beta.partition_broadcast(P)).then_inc(small2_loaded, 16)
                    sp.wait_ge(attn_consts, 2)
                    out_weights(0)

                    def walk(hp, order, last):
                        for o in order:
                            if o[0] == "project" and o[2] == 3:
                                copies(hp, o[1])
                            if o[0] == "gather" and o[1] == 0:
                                sp.wait_ge(group_taken, hp + 1)
                                sp.dma_start(x_row[:], x_tiles[:, bass.ds(hp * GROUP, GROUP)]).then_inc(x_again, 16)
                            if o[0] == "project" and o[1] == BATCH - 1 and o[2] == 5 and not last:
                                sp.wait_ge(misc_ready, n_misc(hp, o[3]) + 1)
                                weights(hp + 1)
                            if o[0] == "y" and o[1:3] == (G - 1, len(y_units) - 1) and not last:
                                sp.wait_ge(misc_ready, n_misc(hp, o[3]) + 1)
                                out_weights(hp + 1)
                        if last:
                            sp.wait_ge(comb_step, PAIRS * COMBINE_STEPS)
                            for p in range(BATCH):
                                sp.wait_ge(y_added, n_y(hp, 2 * p + 1, len(y_units) - 1) + 2)
                                sp.dma_start(out_tiles[:, p * TILES:(p + 1) * TILES],
                                             acc[:, p * TILES:(p + 1) * TILES]).then_inc(stored, 16)
                            sp.wait_ge(stored, 16 * BATCH)

                    run(walk, sp)

                @block.gpsimd
                def _(pool):
                    pool.memset(wo[:], 0.0).then_inc(mask_zeroed, 1)
                    pool.memset(mask[:], 0.0).then_inc(mask_zeroed, 1)
                    for i in range(2):
                        pool.memset(v_hi[i][:, :, :, HEAD:HEAD + 1].bitcast(F32), 1.0).then_inc(mask_zeroed, 1)
                    pool.wait_ge(mask_zeroed, 4)
                    tri = mask[:, SEQ - P:SEQ]
                    pool.affine_select(out=tri, in_=tri, pattern=[[-1, P]], compare_op=ALU.is_ge, fill=MASKED,
                                       base=0, channel_multiplier=1).then_inc(attn_consts, 1)
                    pool.wait_ge(attn_consts, 1)
                    pool.memset(wo[HEAD:HEAD + 1, :, D:D + 1], 1.0).then_inc(attn_consts, 1)
                    n = 2
                    for i in range(2):
                        for s in range(2):
                            pool.wait_ge(attn_consts, n)
                            pool.memset(k_b[i][s][HEAD:HEAD + 2, :].bitcast(F32), 1.0).then_inc(attn_consts, 1)
                            n += 1
                    pool.wait_ge(attn_consts, n)

                    def walk(hp, order, last):
                        for o in order:
                            if o[0] == "gather" and o[1]:
                                n = o[1] - 1
                                pool.wait_ge(group_taken, hp + 1)
                                pool.sem_inc(waited, 1)
                                pool.indirect_dma_start(
                                    two_y[:, n], None, sorted_y,
                                    bass.IndirectOffsetOnAxis(ap=places[:, n:n + 1], axis=0)).then_inc(gathered, 16)
                            if o[0] != "score":
                                continue
                            _, g, c, _ = o
                            slot = (g * CH + c) % RING
                            pool.wait_ge(probs_ready, n_chunk(hp, g, c) + 1 + 2)
                            if DIAG[c]:
                                pool.sem_inc(waited, 1)
                                for tile in (probs[:, slot, 0:P], p_hi[:, slot, 0:P].bitcast(F32)):
                                    out_tile = p_hi[:, slot, 0:P] if tile.tensor.name == "p_hi" else tile
                                    ins = pool.affine_select(out=out_tile, in_=tile, pattern=[[1, P]],
                                                             compare_op=ALU.is_ge, fill=0.0, base=0,
                                                             channel_multiplier=-1)
                                ins.then_inc(diag_masked, 1)
                            if not BY_DVE[c]:
                                if DIAG[c]:
                                    pool.wait_ge(diag_masked, n_diag(hp, g, c) + 1)
                                w = WIDTH[c]
                                pool.tensor_tensor(p_lo[:, slot, 0:w], probs[:, slot, 0:w],
                                                   p_hi[:, slot, 0:w].bitcast(F32),
                                                   ALU.subtract).then_inc(pool_split, 1)

                    run(walk, pool)

                @block.scalar
                def _(act):
                    act.sem_inc(probs_ready, 2)
                    act.sem_inc(heads_out[0], 1)
                    act.sem_inc(heads_out[1], 1)

                    def w_hi(hp):
                        act.wait_ge(qkv_loaded, hp * 16 + 16)
                        act.activation(wqk_hi[:], w_raw[:, 0:2], ACT.Copy).then_inc(wqk_hi_done, 1)

                    def project(hp, p, n, u):
                        i = p % 2
                        act.wait_ge(misc_ready, n_misc(hp, u) + 1)
                        src = misc_ps[u % 2]
                        if n < 4:
                            dst, cols = (q_a, k_a)[n // 2][i], slice(n % 2 * BANK, (n % 2 + 1) * BANK)
                            for s in range(2):
                                act.activation(dst[s][0:HEAD, cols], src[s * HEAD:(s + 1) * HEAD, :],
                                               ACT.Copy).then_inc(hi_done, 1)
                        else:
                            t = (n - 4) * GROUP
                            act.activation(v_hi[i][:, t:t + GROUP, :, 0:HEAD],
                                           src[:].rearrange("p (t s c) -> p t s c", s=2, c=HEAD),
                                           ACT.Copy).then_inc(v_hi_done, 1)

                    def shifts(hp, g, half, u):
                        act.wait_ge(misc_ready, n_misc(hp, u) + 1)
                        dst = q_b[g // 2 % 2][g % 2]
                        act.activation(dst[HEAD:HEAD + 2, half * BANK:(half + 1) * BANK], misc_ps[u % 2][0:2, :],
                                       ACT.Copy).then_inc(shift_done, 1)

                    w_hi(0)

                    def walk(hp, order, last):
                        for o in order:
                            kind, g, c, u = o
                            if kind == "score":
                                half, j, q0 = chunks[c]
                                width = (half + 1) * BANK - q0
                                act.wait_ge(scores_ready, n_chunk(hp, g, c) + 1)
                                act.wait_ge(pv_done, n_chunk(hp, g, c) + 1)
                                for p in (probs, p_hi):
                                    ins = act.activation(p[:, (g * CH + c) % RING, 0:width],
                                                         score_ps[(g * CH + c) % 2][:, 0:width], ACT.Exp,
                                                         scale=SCALE)
                                ins.then_inc(probs_ready, 1)
                            elif kind == "project":
                                project(hp, g, c, u)
                            elif kind == "weights":
                                w_hi(hp + 1)
                            elif kind == "shift":
                                shifts(hp, g, c, u)
                            elif kind == "pv" and c in LAST:
                                half = LAST.index(c)
                                cols = slice(half * BANK, (half + 1) * BANK)
                                act.wait_ge(pv_done, n_chunk(hp, g, c) + 1 + RING)
                                act.activation(heads[:, g % 2, cols], head_ps[0:HEAD + 1, cols],
                                               ACT.Copy).then_inc(heads_out[half], 1)

                    run(walk, act)

                @block.vector
                def _(dve):
                    def w_lo(hp):
                        dve.wait_ge(wqk_hi_done, hp + 1)
                        dve.tensor_tensor(wqk_lo[:], w_raw[:, 0:2], wqk_hi[:].bitcast(F32),
                                          ALU.subtract).then_inc(wqk_split, 1)

                    def project(hp, p, n, u):
                        i = p % 2
                        if n >= 4:
                            t = (n - 4) * GROUP
                            dve.wait_ge(v_hi_done, n_batch(hp, p) * 2 + (n - 3))
                            dve.tensor_tensor(v_lo[i][:, t:t + GROUP],
                                              misc_ps[u % 2][:].rearrange("p (t s c) -> p t s c", s=2, c=HEAD),
                                              v_hi[i][:, t:t + GROUP, :, 0:HEAD].bitcast(F32),
                                              ALU.subtract).then_inc(v_done, 1)
                            return
                        cols = slice(n % 2 * BANK, (n % 2 + 1) * BANK)
                        src = misc_ps[u % 2]
                        for s in range(2):
                            dve.wait_ge(hi_done, n_batch(hp, p) * 8 + (n * 2 + s + 1))
                            hi = (q_a, k_a)[n // 2][i][s][0:HEAD, cols].bitcast(F32)
                            lo = q_a[i][s][HEAD:P, cols] if n < 2 else k_b[i][s][0:HEAD, cols]
                            ins = dve.tensor_tensor(lo, src[s * HEAD:(s + 1) * HEAD, :], hi, ALU.subtract)
                        ins.then_inc(lo_done, 1)

                    def maximum(hp, g, m):
                        t, k0 = max_parts[m]
                        width = min((t + 1) * P - k0, BANK)
                        end = SEQ if (t + 1) * P <= k0 + BANK else SEQ - P
                        dve.wait_ge(max_scores, n_max(hp, g, m) + 1)
                        if g or m >= 2:
                            dve.wait_ge(max_taken, n_max(hp, g, m) - 1)
                        dve.sem_inc(waited, 1)
                        so_far = row_max[:, g % 2, t:t + 1]
                        dve.tensor_tensor_reduce(out=unread[:, m % 2, 0:width], in0=max_ps[:, m % 2, 0:width],
                                                 in1=mask[:, end - width:end], scale=1.0,
                                                 scalar=so_far if k0 else MASKED, op0=ALU.add, op1=ALU.max,
                                                 accum_out=so_far).then_inc(max_taken, 1)

                    def max_hi(hp, g, half):
                        rows = slice(half * GROUP, (half + 1) * GROUP)
                        dve.wait_ge(max_taken, n_max(hp, g, max_parts.index((3, 0) if half == 0 else (7, BANK))) + 1)
                        dve.tensor_scalar(shift[:, g % 2, rows, 0], row_max[:, g % 2, rows], -1.0, None,
                                          ALU.mult).then_inc(max_step, 1)

                    def max_lo(hp, g, half):
                        rows = slice(half * GROUP, (half + 1) * GROUP)
                        dve.wait_ge(max_step, n_half(hp, g, half) + 1)
                        dve.scalar_tensor_tensor(out=shift[:, g % 2, rows, 1], in0=row_max[:, g % 2, rows],
                                                 scalar=-1.0, in1=shift[:, g % 2, rows, 0].bitcast(F32),
                                                 op0=ALU.mult, op1=ALU.subtract).then_inc(max_split, 1)

                    def combine(hp, part):
                        toks, over = bass.ds(hp * GROUP, GROUP), [P, GROUP, D]
                        if part == 0:
                            dve.wait_ge(x_again, hp * 16 + 16)
                            dve.tensor_copy(gsc[:, 0], mean[:, toks])
                            dve.tensor_copy(gsc[:, 1], rstd[:, toks])
                            dve.tensor_copy(gsc[:, 2:4], weights[:, :, toks]).then_inc(comb_step, 1)
                            return
                        dve.wait_ge(comb_step, hp * COMBINE_STEPS + part)
                        if part == 1:
                            for q in range(GROUP):
                                ins = dve.tensor_scalar(x_row[:, q], x_row[:, q], gsc[:, 0, q:q + 1],
                                                        gsc[:, 1, q:q + 1], ALU.subtract, ALU.mult)
                        elif part in (2, 3):
                            if part == 2:
                                dve.wait_ge(gathered, hp * (16 * 2 * GROUP) + 16 * 2 * GROUP)
                            for q in range(GROUP):
                                ins = dve.scalar_tensor_tensor(out=x_row[:, q], in0=two_y[:, (part - 2) * GROUP + q],
                                                               scalar=gsc[:, part, q:q + 1], in1=x_row[:, q],
                                                               op0=ALU.mult, op1=ALU.add)
                        elif part == 4:
                            for q in range(GROUP):
                                ins = dve.bn_stats(gstat[:, q], x_row[:, q])
                        elif part == 5:
                            dve.sem_inc(waited, 1)
                            for q in range(GROUP):
                                ins = dve.bn_aggr(gmom[:, q], gstat[:, q])
                        elif part == 6:
                            ins = dve.tensor_scalar(gvar[:, 0], gmom[:, :, 1], LN_EPS, None, ALU.add)
                        elif part < 7 + RSQRT_STEPS:
                            ins = rsqrt_step(dve, part - 7, gvar[:, 0], gvar[:, 1], gvar[:, 2])
                        elif part == 7 + RSQRT_STEPS:
                            for q in range(GROUP):
                                ins = dve.tensor_scalar(x_row[:, q], x_row[:, q], gmom[:, q, 0:1],
                                                        gvar[:, 1, q:q + 1], ALU.subtract, ALU.mult)
                        elif part == 8 + RSQRT_STEPS:
                            ins = dve.tensor_tensor(x_row[:], x_row[:], fgamma[:].unsqueeze(1).broadcast_to(over),
                                                    ALU.mult)
                        else:
                            dve.tensor_tensor(x_row[:], x_row[:], fbeta[:].unsqueeze(1).broadcast_to(over),
                                              ALU.add).then_inc(comb_step, 1)
                            dve.wait_ge(comb_step, hp * COMBINE_STEPS + (part + 1))
                            ins = dve.tensor_tensor(acc[:, toks], acc[:, toks], x_row[:], ALU.add)
                        ins.then_inc(comb_step, 1)

                    def denominators(hp, g, n, u):
                        t0, tiles = y_units[n]
                        src = misc_ps[u % 2][:, 0:tiles * (D + 1)].rearrange("p (t d) -> p t d", t=tiles)
                        dve.wait_ge(misc_ready, n_misc(hp, u) + 1)
                        dve.reciprocal(rden[:, u % 2, 0:tiles], src[:, :, D]).then_inc(recip_done, 1)

                    def add_y(hp, g, n, u):
                        t0, tiles = y_units[n]
                        src = misc_ps[u % 2][:, 0:tiles * (D + 1)].rearrange("p (t d) -> p t d", t=tiles)
                        dve.wait_ge(recip_done, n_y(hp, g, n) + 1)
                        for t in range(tiles):
                            row = acc[:, g // 2 * TILES + t0 + t]
                            ins = dve.scalar_tensor_tensor(out=row, in0=src[:, t, 0:D], scalar=rden[:, u % 2, t:t + 1],
                                                           in1=row, op0=ALU.mult, op1=ALU.add)
                        ins.then_inc(y_added, 1)

                    dve.sem_inc(pv_done, RING)
                    dve.sem_inc(y_added, 1)
                    w_lo(0)
                    dve.wait_ge(attn_consts, 1)
                    dve.wait_ge(small2_loaded, 32)

                    def walk(hp, order, last):
                        for o in order:
                            kind, g, c, u = o
                            if kind == "max":
                                maximum(hp, g, c)
                            elif kind == "project":
                                project(hp, g, c, u)
                            elif kind == "weights":
                                w_lo(hp + 1)
                            elif kind == "y":
                                denominators(hp, g, c, u)
                            elif kind == "add":
                                add_y(hp, g, c, u)
                            elif kind == "max_hi":
                                max_hi(hp, g, c)
                            elif kind == "max_lo":
                                max_lo(hp, g, c)
                            elif kind == "gather" and g == 0:
                                dve.tensor_copy(places[:].rearrange("p (n q) -> p n q", n=2),
                                                slots[:, :, bass.ds(hp * GROUP, GROUP)]).then_inc(group_taken, 1)
                            elif kind == "combine":
                                combine(hp, g)
                            elif kind == "low" and BY_DVE[c]:
                                half, j, q0 = chunks[c]
                                slot, width = (g * CH + c) % RING, (half + 1) * BANK - q0
                                dve.wait_ge(diag_masked, n_diag(hp, g, c) + 1)
                                dve.tensor_tensor(p_lo[:, slot, 0:width], probs[:, slot, 0:width],
                                                  p_hi[:, slot, 0:width].bitcast(F32),
                                                  ALU.subtract).then_inc(dve_split, 1)

                    run(walk, dve)

                @block.tensor
                def _(pe):
                    def misc_read(hp, kind, g, n):
                        if kind == "project" and n < 4:
                            pe.wait_ge(lo_done, n_batch(hp, g) * 4 + (n + 1))
                        elif kind == "project":
                            pe.wait_ge(v_done, n_batch(hp, g) * 2 + (n - 3))
                        elif kind == "shift":
                            pe.wait_ge(shift_done, n_half(hp, g, n) + 1)
                        else:
                            pe.wait_ge(y_added, n_y(hp, g, n) + 2)

                    def misc_bank(hp, u):
                        if u >= 2:
                            misc_read(hp, *units[u - 2])
                        if 0 <= u - MISC0 < 2:
                            kind, g, n = misc_units(plan(False))[u - MISC0 - 2]
                            misc_read(hp, kind, g - (BATCH if kind == "project" else G), n)
                        return misc_ps[u % 2]

                    def project(hp, p, n, u):
                        toks = (p % BATCH) * SEQ
                        dst = misc_bank(hp, u)
                        if n < 4:
                            w = n // 2
                            cols = slice(toks + n % 2 * BANK, toks + (n % 2 + 1) * BANK)
                            if n == 0:
                                pe.wait_ge(wqk_split, hp + (p // BATCH + 1))
                            pe.matmul(dst[:], wqk_hi[:, w], nT_hi[:, cols], start=True, stop=False)
                            pe.matmul(dst[:], wqk_hi[:, w], nT_lo[:, cols], start=False, stop=False)
                            ins = pe.matmul(dst[:], wqk_lo[:, w], nT_hi[:, cols], start=False, stop=True)
                        else:
                            for q in range(GROUP):
                                t0 = toks + ((n - 4) * GROUP + q) * P
                                ins = pe.matmul(dst[:, q * P:(q + 1) * P], nT[:, t0:t0 + P], w_raw[:, 2],
                                                start=True, stop=True)
                        ins.then_inc(misc_ready, 1)

                    def max_scores_of(hp, g, m):
                        i, s = g // 2 % 2, g % 2
                        t, k0 = max_parts[m]
                        k1 = min((t + 1) * P, k0 + BANK)
                        if m == 0 and s == 0:
                            pe.wait_ge(copies_done, n_batch(hp, g // 2) * 64 + 64)
                            pe.wait_ge(lo_done, n_batch(hp, g // 2) * 4 + 4)
                        if g or m >= 2:
                            pe.wait_ge(max_taken, n_max(hp, g, m) - 1)
                        pe.matmul(max_ps[:, m % 2, 0:k1 - k0], q_a[i][s][:, t * P:(t + 1) * P],
                                  k_a[i][s][:, k0:k1], start=True, stop=True).then_inc(max_scores, 1)

                    def shifts(hp, g, half, u):
                        dst = misc_bank(hp, u)
                        pe.wait_ge(max_split, n_half(hp, g, half) + 1)
                        for q in range(GROUP):
                            ins = pe.transpose(dst[0:2, q * P:(q + 1) * P],
                                               shift[:, g % 2, half * GROUP + q, :].bitcast(F32), ident[:])
                        ins.then_inc(misc_ready, 1)

                    def score(hp, g, c):
                        half, j, q0 = chunks[c]
                        i, s = g // 2 % 2, g % 2
                        dst = score_ps[(g * CH + c) % 2][:, 0:(half + 1) * BANK - q0]
                        keys, qs = slice(j * P, (j + 1) * P), slice(q0, (half + 1) * BANK)
                        pe.wait_ge(probs_ready, n_chunk(hp, g, c) + 1)
                        if j == 0:
                            pe.wait_ge(shift_done, n_half(hp, g, half) + 1)
                        pe.matmul(dst, k_a[i][s][:, keys], q_a[i][s][:, qs], start=True, stop=False)
                        pe.matmul(dst, k_b[i][s][:, keys], q_b[i][s][:, qs], start=False,
                                  stop=True).then_inc(scores_ready, 1)

                    def values(hp, g, c):
                        half, j, q0 = chunks[c]
                        i, s = g // 2 % 2, g % 2
                        width = (half + 1) * BANK - q0
                        if BY_DVE[c]:
                            pe.wait_ge(dve_split, n_dve(hp, g, c) + 1)
                        else:
                            pe.wait_ge(pool_split, n_pool(hp, g, c) + 1)
                        if j == 0:
                            pe.wait_ge(heads_out[half], hp * G + (g + 1))
                        if c == 0:
                            pe.wait_ge(v_done, n_batch(hp, g // 2) * 2 + 2)
                        slot, cols = (g * CH + c) % RING, slice(q0, (half + 1) * BANK)
                        pe.matmul(head_ps[0:HEAD + 1, cols], v_hi[i][:, j, s], p_hi[:, slot, 0:width],
                                  start=(j == 0), stop=False)
                        pe.matmul(head_ps[0:HEAD, cols], v_lo[i][:, j, s], p_hi[:, slot, 0:width],
                                  start=False, stop=False)
                        pe.matmul(head_ps[0:HEAD + 1, cols], v_hi[i][:, j, s], p_lo[:, slot, 0:width],
                                  start=False, stop=c in LAST).then_inc(pv_done, 1)

                    def project_out(hp, g, n, u):
                        t0, tiles = y_units[n]
                        dst = misc_bank(hp, u)
                        if n == 0:
                            pe.wait_ge(heads_out[0], hp * G + (g + 2))
                            pe.wait_ge(heads_out[1], hp * G + (g + 2))
                            if g == 0:
                                pe.wait_ge(wout_loaded, hp * 16 + 16)
                        for t in range(tiles):
                            q0 = (t0 + t) * P
                            ins = pe.matmul(dst[:, t * (D + 1):(t + 1) * (D + 1)], heads[:, g % 2, q0:q0 + P],
                                            wo[:, g % 2], start=True, stop=True)
                        ins.then_inc(misc_ready, 1)

                    units = []
                    pe.wait_ge(attn_consts, 6)

                    def walk(hp, order, last):
                        units[:] = first_units + ([] if order is before_loop else misc_units(order))
                        for kind, g, c, u in order:
                            if kind == "score":
                                score(hp, g, c)
                            elif kind == "max":
                                max_scores_of(hp, g, c)
                            elif kind == "project":
                                project(hp, g, c, u)
                            elif kind == "shift":
                                shifts(hp, g, c, u)
                            elif kind == "pv":
                                values(hp, g, c)
                            elif kind == "y":
                                project_out(hp, g, c, u)

                    run(walk, pe)


_INS = ['L0_attn_x', 'L0_attn_gamma', 'L0_attn_w_qkv', 'L0_attn_w_out', 'L0_ffn_Wr', 'L0_ffn_br', 'L0_ffn_W1',
        'L0_ffn_b1', 'L0_ffn_W2', 'L0_ffn_b2', 'L0_ffn_gamma', 'L0_ffn_beta']
_OUTS = [((4, 1024, 128), 'float32')]


def kernel(**inputs):
    import numpy as _np
    import concourse.bacc as _bacc
    from concourse import mybir as _mybir
    from concourse.bass_utils import run_bass_kernel_spmd as _run

    nc = _bacc.Bacc("TRN2", target_bir_lowering=False, num_devices=1)
    arrays, args = {}, []
    for name in _INS:
        a = _np.ascontiguousarray(inputs[name])
        arrays[f"in_{name}_dram"] = a
        args.append(nc.dram_tensor(f"in_{name}_dram", a.shape, _mybir.dt.from_np(a.dtype), kind="ExternalInput").ap())
    for i, (shape, dtype) in enumerate(_OUTS):
        dt = _mybir.dt.from_np(_np.dtype(dtype))
        args.append(nc.dram_tensor(f"out_{i}_dram", shape, dt, kind="ExternalOutput").ap())
    attention_and_experts(nc, *args)
    r = _run(nc, [arrays], core_ids=[0])
    got = tuple(r.results[0][f"out_{i}_dram"] for i in range(len(_OUTS)))
    return got[0]
```
